# Optimizing a Trainium2 kernel written in Bass

```python
import numpy as np
import jax
import jax.numpy as jnp

def _softmax(x, axis=-1):
    return jax.nn.softmax(x, axis=axis)

def _gelu(x):
    return jax.nn.gelu(x, approximate=True)

def _silu(x):
    return jax.nn.silu(x)

def _sigmoid(x):
    return jax.nn.sigmoid(x)

def _layernorm(x, axis=-1, eps=1e-05):
    m = jnp.mean(x, axis=axis, keepdims=True)
    v = jnp.var(x, axis=axis, keepdims=True)
    return (x - m) / jnp.sqrt(v + eps)

def _scatter_add(tgt, idx, src, axis=0):
    return tgt.at[idx].add(src)

def _segment_sum(src, seg, n):
    return jax.ops.segment_sum(src, seg, n)
kernel_name = 'mk_rec_standalone_d1_rec_r8_611a51'

def setup_inputs(seed: int=0):
    np.random.seed(seed)
    _w = jnp.asarray

    def _rec_inputs():
        import jax
        import jax.numpy as jnp
        _rk = jax.random.key(seed)
        r_history_mask = jax.random.randint(jax.random.fold_in(_rk, 1), (512, 50), 0, 2, jnp.int32)
        return r_history_mask
    r_history_mask = _rec_inputs()

    def _L0_rec_setup():
        import jax, jax.numpy as jnp
        import numpy as np
        D = 256
        A = 64
        S = 50
        B = 512
        H = 4
        HD = D // H

        def prelu(x, a):
            return jnp.where(x >= 0, x, a * x)
        key = jax.random.key(seed)
        ks = jax.random.split(key, 16)
        s = 0.02
        return {'query': jax.random.normal(ks[0], (B, D), jnp.float32), 'history': jax.random.normal(ks[1], (B, S, D), jnp.float32), 'history_mask': jax.random.randint(ks[2], (B, S), 0, 2, jnp.int32), 'W1': jax.random.normal(ks[3], (A, 4 * D), jnp.float32) * s, 'b1': jnp.zeros((A,), jnp.float32), 'a1': jnp.full((), 0.25, jnp.float32), 'W2': jax.random.normal(ks[4], (A, A), jnp.float32) * s, 'b2': jnp.zeros((A,), jnp.float32), 'a2': jnp.full((), 0.25, jnp.float32), 'W3': jax.random.normal(ks[5], (1, A), jnp.float32) * s, 'b3': jnp.zeros((1,), jnp.float32), 'in_w': jax.random.normal(ks[6], (3 * D, D), jnp.float32) * s, 'in_b': jnp.zeros((3 * D,), jnp.float32), 'out_w': jax.random.normal(ks[7], (D, D), jnp.float32) * s, 'out_b': jnp.zeros((D,), jnp.float32), 'Wo': jax.random.normal(ks[8], (D, 2 * D), jnp.float32) * s, 'bo': jnp.zeros((D,), jnp.float32), 'ln_w': jnp.ones((D,), jnp.float32), 'ln_b': jnp.zeros((D,), jnp.float32), 'ao': jnp.full((), 0.25, jnp.float32)}
    _L0_rec_all = _L0_rec_setup()
    _L0_rec_in = {k: v for k, v in _L0_rec_all.items() if k in ('query', 'history', 'W1', 'b1', 'a1', 'W2', 'b2', 'a2', 'W3', 'b3', 'in_w', 'in_b', 'out_w', 'out_b', 'Wo', 'bo', 'ln_w', 'ln_b', 'ao')}
    del _L0_rec_all
    return {'r_history_mask': r_history_mask, 'L0_rec_query': _L0_rec_in['query'], 'L0_rec_history': _L0_rec_in['history'], 'L0_rec_W1': _L0_rec_in['W1'], 'L0_rec_b1': _L0_rec_in['b1'], 'L0_rec_a1': _L0_rec_in['a1'], 'L0_rec_W2': _L0_rec_in['W2'], 'L0_rec_b2': _L0_rec_in['b2'], 'L0_rec_a2': _L0_rec_in['a2'], 'L0_rec_W3': _L0_rec_in['W3'], 'L0_rec_b3': _L0_rec_in['b3'], 'L0_rec_in_w': _L0_rec_in['in_w'], 'L0_rec_in_b': _L0_rec_in['in_b'], 'L0_rec_out_w': _L0_rec_in['out_w'], 'L0_rec_out_b': _L0_rec_in['out_b'], 'L0_rec_Wo': _L0_rec_in['Wo'], 'L0_rec_bo': _L0_rec_in['bo'], 'L0_rec_ln_w': _L0_rec_in['ln_w'], 'L0_rec_ln_b': _L0_rec_in['ln_b'], 'L0_rec_ao': _L0_rec_in['ao']}

def reference(r_history_mask, L0_rec_query, L0_rec_history, L0_rec_W1, L0_rec_b1, L0_rec_a1, L0_rec_W2, L0_rec_b2, L0_rec_a2, L0_rec_W3, L0_rec_b3, L0_rec_in_w, L0_rec_in_b, L0_rec_out_w, L0_rec_out_b, L0_rec_Wo, L0_rec_bo, L0_rec_ln_w, L0_rec_ln_b, L0_rec_ao):
    import jax
    import jax.numpy as jnp

    def _L0_rec_ref(query, history, history_mask, W1, b1, a1, W2, b2, a2, W3, b3, in_w, in_b, out_w, out_b, Wo, bo, ln_w, ln_b, ao):
        import jax, jax.numpy as jnp
        import numpy as np
        D = 256
        A = 64
        S = 50
        B = 512
        H = 4
        HD = D // H

        def prelu(x, a):
            return jnp.where(x >= 0, x, a * x)
        mask = history_mask.astype(bool)
        neg_inf = jnp.float32(-jnp.inf)
        qe = jnp.broadcast_to(query[:, None, :], history.shape)
        act_in = jnp.concatenate([qe, history, qe - history, qe * history], axis=-1)
        h = prelu(act_in @ W1.T + b1, a1)
        h = prelu(h @ W2.T + b2, a2)
        scores = (h @ W3.T + b3)[..., 0]
        scores = jnp.where(mask, scores, neg_inf)
        attn_w = jax.nn.softmax(scores, axis=-1)
        interest = jnp.einsum('bs,bsd->bd', attn_w, history)
        Wq, Wk, Wv = (in_w[:D], in_w[D:2 * D], in_w[2 * D:])
        bq, bk, bv = (in_b[:D], in_b[D:2 * D], in_b[2 * D:])
        q = (query @ Wq.T + bq).reshape(B, H, 1, HD)
        k = (history @ Wk.T + bk).reshape(B, S, H, HD).transpose(0, 2, 1, 3)
        v = (history @ Wv.T + bv).reshape(B, S, H, HD).transpose(0, 2, 1, 3)
        logits = jnp.einsum('bhqd,bhkd->bhqk', q, k) / jnp.sqrt(jnp.float32(HD))
        logits = jnp.where(mask[:, None, None, :], logits, neg_inf)
        p = jax.nn.softmax(logits, axis=-1)
        mha = jnp.einsum('bhqk,bhkd->bhqd', p, v).reshape(B, D)
        mha = mha @ out_w.T + out_b
        combined = jnp.concatenate([interest, mha], axis=-1)
        z = combined @ Wo.T + bo
        mu = jnp.mean(z, axis=-1, keepdims=True)
        var = jnp.mean(jnp.square(z - mu), axis=-1, keepdims=True)
        z = (z - mu) * jax.lax.rsqrt(var + 1e-05) * ln_w + ln_b
        return prelu(z, ao)
    y = _L0_rec_ref(L0_rec_query, L0_rec_history, r_history_mask, L0_rec_W1, L0_rec_b1, L0_rec_a1, L0_rec_W2, L0_rec_b2, L0_rec_a2, L0_rec_W3, L0_rec_b3, L0_rec_in_w, L0_rec_in_b, L0_rec_out_w, L0_rec_out_b, L0_rec_Wo, L0_rec_bo, L0_rec_ln_w, L0_rec_ln_b, L0_rec_ao)
    return y

_drawn_inputs = setup_inputs


def setup_inputs(seed=0):
    import zlib

    import numpy as np

    out = dict(_drawn_inputs(seed))
    spreads = {'L0_rec_b1': (0.0, 0.8),
     'L0_rec_b2': (0.0, 0.8),
     'L0_rec_in_b': (0.0, 0.1),
     'L0_rec_out_b': (0.0, 0.1),
     'L0_rec_bo': (0.0, 0.1),
     'L0_rec_ln_w': (1.0, 0.2),
     'L0_rec_ln_b': (0.0, 0.1)}
    factors = {'L0_rec_query': 8.0, 'L0_rec_W1': 8.0, 'L0_rec_W2': 8.0, 'L0_rec_W3': 8.0}
    for name, (base, spread) in spreads.items():
        noise = np.random.default_rng([zlib.crc32(name.encode()), seed]).standard_normal(out[name].shape)
        drawn = base * np.exp(spread * noise) if base else spread * noise
        out[name] = jnp.asarray(drawn.astype(out[name].dtype))
    for name, factor in factors.items():
        out[name] = (out[name] * factor).astype(out[name].dtype)
    return out
```

```python
from contextlib import ExitStack

import concourse.bass as bass
from concourse import mybir

F32 = mybir.dt.float32
I32 = mybir.dt.int32
ALU = mybir.AluOpType
ACT = mybir.ActivationFunctionType

BIG = 1e30
EPS = 1e-5


def at_least(engine, semaphore, count):
    if isinstance(count, int) and count <= 0:
        return
    engine.wait_ge(semaphore, count)


def rec_kernel(nc, mask, query, history, W1, b1, a1, W2, b2, a2, W3, b3, in_w, in_b, out_w, out_b,
               Wo, bo, ln_w, ln_b, ao, out):
    B, S, D = history.shape
    A = W2.shape[0]
    H = 4
    HD = D // H
    P = 128
    C = D // P
    GB = 8
    GR = GB * S
    TR = 2 * S
    NK = GR // TR
    QB = 4 * GB
    QT = 4 * NK
    NQ = B // QB
    RING = 4
    BB = B // P
    PW = 48
    assert (C, A, HD, TR, NQ % RING) == (2, 64, 64, 100, 0)

    hist_v = history.rearrange("(q r t e) s d -> q r (e s) t d", r=2, t=QT // 2, e=2)

    with ExitStack() as ctx:
        def sb(name, shape, dt=F32):
            return ctx.enter_context(nc.sbuf_tensor(name, shape, dt))

        def sem(name):
            return ctx.enter_context(nc.semaphore(name))

        hist = sb("hist", [P, RING, QT, D])
        hT = sb("hT", [P, 2, 2, C, 2 * GR])
        qhT = sb("qhT", [P, 2, C, 2 * GR])
        h1 = sb("h1", [P, 2, GR])
        h2 = sb("h2", [P, 2, GR])
        log_t = sb("log_t", [P, GR])
        log_p = sb("log_p", [P, GR])
        din_t = sb("din_t", [64, GR])
        din_p = sb("din_p", [64, GR])
        small = sb("small", [P, 8])
        p_w = sb("p_w", [P, QT, PW])
        pooled = sb("pooled", [P, 2, D])
        headT = sb("headT", [P, C, B * H])
        interestT = sb("interestT", [P, C, B])
        kq = sb("kq", [P, C, B * H])
        kq_quad = sb("kq_quad", [P, 2, C, P])
        mask_log = sb("mask_log", [P, 2, GR])
        mask_din = sb("mask_din", [64, 2, GR])
        own_log = sb("own_log", [P, NQ, S])
        own_din = sb("own_din", [64, NQ, S])
        other_log = sb("other_log", [P, GB])
        other_din = sb("other_din", [64, GB])
        ident = sb("ident", [P, P])
        ones = sb("ones", [P, P])
        mask_i = sb("mask_i", [QB, NQ, S], I32)
        mask_f = sb("mask_f", [QB, NQ, S])
        to_log = sb("to_log", [QB, GB // 2, GB, H])
        to_din = sb("to_din", [QB, 4, 16])
        of_group = sb("of_group", [QB, GB])
        query_n = hist[:, RING - 1, 0:4, :]
        inw_n = hist[:, RING - 1, 4:10, :]
        outw_n = hist[:, RING - 1, 10:12, :]
        wo_n = hist[:, RING - 1, 12:16, :].rearrange("p (t x) d -> p t (x d)", t=C)
        qT = sb("qT", [P, C, B])
        w1_n = sb("w1_n", [A, 4, D])
        w1_c = sb("w1_c", [A, 2, D])
        w1T = sb("w1T", [P, 2 * C, A])
        w1uT = sb("w1uT", [P, C, 2, A])
        u = sb("u", [P, 2 * NQ, GB])
        b1_c = sb("b1_c", [P, 1])
        b2_c = sb("b2_c", [P, 1])
        b3_c = sb("b3_c", [64, 1])
        a1_c = sb("a1_c", [P, 1])
        a2_c = sb("a2_c", [P, 1])
        ao_c = sb("ao_c", [P, 1])
        sign = sb("sign", [P, 8])
        b1_s = sb("b1_s", [P, 1])
        b2_s = sb("b2_s", [P, 1])
        w2_n = sb("w2_n", [P, P])
        w2T = sb("w2T", [P, P])
        w3_c = sb("w3_c", [P, 1])
        w3_x = sb("w3_x", [P, 32])
        inb_c = sb("inb_c", [P, 3 * C])
        bk_x = sb("bk_x", [P, C, H])
        wqT = sb("wqT", [P, C, D])
        wvT = sb("wvT", [P, C, D])
        early = qhT[:, :, :, :].rearrange("p r c n -> p (r c n)")
        q_x = early[:, 0:2 * C * B].rearrange("p (r c b) -> p r c b", r=2, c=C)
        q_e = early[:, 2 * C * B:3 * C * B].rearrange("p (c b) -> p c b", c=C)
        qbk_r = sb("qbk_r", [H, QB, NQ])
        qbk = sb("qbk", [P, NQ])
        outwT = sb("outwT", [P, C, D])
        outb_c = sb("outb_c", [P, C])
        woT = sb("woT", [P, 2 * C, D])
        bo_b = sb("bo_b", [P, D])
        lnw_b = sb("lnw_b", [P, D])
        lnb_b = sb("lnb_b", [P, D])
        late = hT[:, :, :, :, :].rearrange("p k r c n -> p (k r c n)")
        vT, mhaT = (late[:, i * C * B:(i + 1) * C * B].rearrange("p (c b) -> p c b", c=C) for i in range(2))
        z, zn = (late[:, i * C * B:(i + 1) * C * B].rearrange("p (j d) -> p j d", j=BB) for i in (2, 3))
        stats = sb("stats", [P, BB, 6])
        moments = sb("moments", [P, BB, 2])
        rstd = sb("rstd", [P, BB, 2])
        minus_half = sb("minus_half", [P, 1])

        psum = ctx.enter_context(nc.psum_tensor("psum", [P, 8, 512], F32))
        bank = [psum[:, i, :] for i in range(8)]

        def view(t, offset, dims, parts=P, start=0):
            base = t[start:start + parts]
            free = 1
            for n in t.shape[1:]:
                free *= n
            return bass.AP(base.tensor, base.offset + offset, [[free, parts]] + [list(d) for d in dims])

        ld_query, ld_w1, ld_inw, ld_mask = sem("ld_query"), sem("ld_w1"), sem("ld_inw"), sem("ld_mask")
        ld_small, ld_late, ld_w2 = sem("ld_small"), sem("ld_late"), sem("ld_w2")
        ld_hist = [[sem(f"ld_hist{k}{r}") for r in range(2)] for k in range(RING)]
        consts, cleared = sem("consts"), sem("cleared")
        pre_pe, pre_dve, pre_act, prepared = sem("pre_pe"), sem("pre_dve"), sem("pre_act"), sem("prepared")
        qbk_moved = sem("qbk_moved")
        turned = sem("turned")
        hT_ready = sem("hT_ready")
        qhT_ready = sem("qhT_ready")
        layer1 = sem("layer1")
        h1_sum = sem("h1_sum")
        h1_ready = sem("h1_ready")
        layer2 = sem("layer2")
        h2_sum = sem("h2_sum")
        h2_ready = sem("h2_ready")
        signs = sem("signs")
        logits = sem("logits")
        scores = sem("scores")
        log_masked, din_masked = sem("log_masked"), sem("din_masked")
        log_exp, din_exp = sem("log_exp"), sem("din_exp")
        log_probs, din_probs = sem("log_probs"), sem("din_probs")
        recips = sem("recips")
        log_pT, din_pT = sem("log_pT"), sem("din_pT")
        log_w, din_w = sem("log_w"), sem("din_w")
        pool_done = sem("pool_done")
        pooled_ready = sem("pooled_ready")
        pooledT = sem("pooledT")
        pooledT_ready = sem("pooledT_ready")
        quad_kq = sem("quad_kq")
        quad_masks = sem("quad_masks")
        v_done, v_ready, mha_done, mha_ready = sem("v_done"), sem("v_ready"), sem("mha_done"), sem("mha_ready")
        z_done, z_ready, z_stats, z_moments = sem("z_done"), sem("z_ready"), sem("z_stats"), sem("z_moments")
        z_eps, z_rstd, z_norm, z_scaled, z_shifted = (
            sem("z_eps"), sem("z_rstd"), sem("z_norm"), sem("z_scaled"), sem("z_shifted"))
        z_below, y_ready, stored = sem("z_below"), sem("y_ready"), sem("stored")

        N_SMALL, N_LATE = 10, 8
        PRE_PE, PRE_DVE, PRE_ACT = 25, 19, 15

        block = ctx.enter_context(nc.Block())

        @block.sync
        def _(sp):
            sp.dma_start(query_n, query.rearrange("(j p) d -> p j d", p=P)).then_inc(ld_query, 16)

            def load(q, k):
                for r in range(2):
                    at_least(sp, pool_done, q - RING + 1)
                    sp.dma_start(hist[0:TR, k, r * (QT // 2):(r + 1) * (QT // 2), :],
                                 hist_v[q, r]).then_inc(ld_hist[k][r], 16)

            sp.dma_start(w1_n[:, :, :], W1.rearrange("a (f d) -> a f d", f=4)).then_inc(ld_w1, 16)
            for r in range(2):
                sp.dma_start(inw_n[:, 2 * r:2 * r + 2, :],
                             in_w.rearrange("(t p) d -> p t d", p=P)[:, 2 * r:2 * r + 2, :]).then_inc(ld_inw, 16)
            load(0, 0)
            sp.dma_start(inw_n[:, 4:6, :],
                         in_w.rearrange("(t p) d -> p t d", p=P)[:, 4:6, :]).then_inc(ld_late, 16)
            sp.dma_start(outw_n[:, :, :], out_w.rearrange("(t p) d -> p t d", p=P)).then_inc(ld_late, 16)
            sp.dma_start(wo_n[:, :, :], Wo.rearrange("(t p) d -> p t d", p=P)).then_inc(ld_late, 16)
            for k in range(1, RING - 1):
                load(k, k)
            sp.wait_ge(pre_pe, PRE_PE)
            load(RING - 1, RING - 1)
            with sp.Fori(1, NQ // RING) as it:
                for k in range(RING):
                    load(it * RING + k, k)
            for j in range(BB):
                sp.wait_ge(y_ready, j + 1)
                sp.dma_start(out[j * P:(j + 1) * P, :], z[:, j, :]).then_inc(stored, 16)
            sp.wait_ge(stored, 16 * BB)


        @block.gpsimd
        def _(pool):
            pool.memset(ident[:, :], 0.0).then_inc(cleared, 1)
            pool.memset(to_log[:, :, :, :], 0.0).then_inc(cleared, 1)
            pool.memset(to_din[:, :, :], 0.0).then_inc(cleared, 1)
            pool.memset(of_group[:, :], 0.0).then_inc(cleared, 1)
            pool.wait_ge(cleared, 4)
            pool.affine_select(out=ident[:, :], in_=ident[:, :], compare_op=ALU.not_equal, fill=1.0, base=0,
                               pattern=[[-1, P]], channel_multiplier=1).then_inc(consts, 1)
            pool.affine_select(out=to_log[:, :, :, :], in_=to_log[:, :, :, :], compare_op=ALU.not_equal, fill=1.0,
                               base=0, pattern=[[-GB, 4], [-1, GB], [0, H]], channel_multiplier=1).then_inc(consts, 1)
            pool.affine_select(out=to_din[:, :, 0:GB], in_=to_din[:, :, 0:GB], compare_op=ALU.not_equal, fill=1.0,
                               base=0, pattern=[[-GB, 4], [-1, GB]], channel_multiplier=1).then_inc(consts, 1)
            for g in range(4):
                ins = pool.affine_select(out=of_group[:, :], in_=of_group[:, :], compare_op=ALU.not_equal, fill=1.0,
                                         base=-GB * g, pattern=[[-1, GB]], channel_multiplier=1)
                ins.then_inc(consts, 1)
                pool.wait_ge(consts, 4 + g)

            def quad(q, k):
                at_least(pool, logits, q - 1)
                pool.tensor_copy(kq_quad[:, k % 2, :, :],
                                 kq[:, :, bass.ds(q * P, P)]).then_inc(quad_kq, 1)
                at_least(pool, log_masked, q - 1)
                at_least(pool, din_masked, q - 1)
                for m, own, other, n in ((mask_log, own_log, other_log, P), (mask_din, own_din, other_din, 64)):
                    pool.tensor_tensor(m[:, k % 2, :].rearrange("p (e s) -> p e s", s=S),
                                       other[:, :].unsqueeze(2).to_broadcast([n, GB, S]),
                                       own[:, bass.ds(q, 1), :].to_broadcast([n, GB, S]),
                                       ALU.add).then_inc(quad_masks, 1)

            pool.wait_ge(pre_dve, PRE_DVE)
            pool.wait_ge(pre_act, PRE_ACT)
            for k in range(RING):
                quad(k, k)
            with pool.Fori(1, NQ // RING) as it:
                for k in range(RING):
                    quad(it * RING + k, k)
            pool.memset(minus_half[:, :], -0.5).then_inc(z_eps, 1)
            pool.wait_ge(z_eps, 1)
            for j in range(BB):
                pool.wait_ge(z_moments, 2 * j + 2)
                pool.tensor_tensor(rstd[:, j, 1:2], rstd[:, j, 0:1], minus_half[:, :], ALU.pow).then_inc(z_rstd, 1)

        @block.tensor
        def _(pe):
            n = [0]

            def done(ins):
                n[0] += 1
                ins.then_inc(pre_pe, 1)
                return n[0]

            def mm(o, l, r, first=True, last=True):
                return pe.matmul(o, l, r, start=first, stop=last, skip_group_check=True)

            pe.wait_ge(consts, 7)
            pe.wait_ge(ld_query, 16)
            for c in range(C):
                for j in range(BB):
                    ins = pe.transpose(bank[c][:, j * P:(j + 1) * P], query_n[:, j, c * P:(c + 1) * P], ident[:, :])
                done(ins)
            pe.wait_ge(ld_inw, 32)
            for c in range(C):
                for t in range(C):
                    ins = pe.transpose(bank[2][:, c * D + t * P:c * D + (t + 1) * P],
                                       inw_n[:, t, c * P:(c + 1) * P], ident[:, :])
            done(ins)
            pe.wait_ge(prepared, 2)
            for i, src in enumerate((w1_c[:, 1, 0:P], w1_c[:, 1, P:D], w1_n[:, 3, 0:P], w1_n[:, 3, P:D],
                                     w1_c[:, 0, 0:P], w1_c[:, 0, P:D])):
                ins = pe.transpose(bank[3][:, i * A:(i + 1) * A], src, ident[0:A, 0:A])
            done(ins)
            pe.wait_ge(ld_w2, 32)
            done(pe.transpose(bank[4][:, 0:P], w2_n[:, :], ident[:, :]))
            pe.wait_ge(pre_act, 3)
            for t in range(C):
                for c in range(C):
                    ins = mm(bank[5 + t][:, :], wqT[:, c, t * P:(t + 1) * P], qT[:, c, :], c == 0, c == C - 1)
                done(ins)
            pe.wait_ge(pre_dve, 3)
            for c in range(C):
                ins = mm(bank[7][:, :], w1uT[:, c, :, :].rearrange("p a b -> p (a b)"), qT[:, c, :],
                         c == 0, c == C - 1)
            done(ins)
            pe.wait_ge(pre_dve, 9)
            for t in range(C):
                ins = mm(bank[0][0:H, :], bk_x[:, t, :], q_e[:, t, :], t == 0, t == C - 1)
            done(ins)
            for h in range(H):
                for c in range(C):
                    i = h * C + c
                    if i >= 2:
                        pe.wait_ge(pre_act, 3 + i - 1)
                    else:
                        pe.wait_ge(pre_dve, 9)
                    done(mm(bank[1 + i % 2][:, :], inw_n[:, C + h // 2, c * P:(c + 1) * P], q_x[:, h % 2, h // 2, :]))
            pe.wait_ge(pre_dve, 10)
            half = NQ // 2
            log_l, din_l = (t[:].rearrange(r) for t, r in (
                (to_log, "b g e h -> b (g e h)"), (to_din, "b g e -> b (g e)")))
            mm(bank[3][:, half * S:half * S + GB], log_l, of_group[:, :])
            mm(bank[5][0:64, half * S:half * S + GB], din_l, of_group[:, :])
            for i in range(2):
                done(mm(bank[3 + i][:, 0:half * S], log_l,
                        mask_f[:, i * half:(i + 1) * half, :].rearrange("b q s -> b (q s)")))
            for i in range(2):
                done(mm(bank[5 + i][0:64, 0:half * S], din_l,
                        mask_f[:, i * half:(i + 1) * half, :].rearrange("b q s -> b (q s)")))
            pe.wait_ge(ld_late, 16 * N_LATE)
            pe.wait_ge(pre_dve, 12)
            for c in range(C):
                for t in range(C):
                    ins = pe.transpose(bank[7][:, c * D + t * P:c * D + (t + 1) * P],
                                       inw_n[:, 2 * C + t, c * P:(c + 1) * P], ident[:, :])
            done(ins)
            pe.wait_ge(pre_act, 11)
            for c in range(C):
                for t in range(C):
                    ins = pe.transpose(bank[1][:, c * D + t * P:c * D + (t + 1) * P],
                                       outw_n[:, t, c * P:(c + 1) * P], ident[:, :])
            done(ins)
            pe.wait_ge(pre_dve, 13)
            for i in range(2):
                for c in range(C):
                    for t in range(C):
                        ins = pe.transpose(bank[(2, 0)[i]][:, c * D + t * P:c * D + (t + 1) * P],
                                           wo_n[:, t, (2 * i + c) * P:(2 * i + c + 1) * P], ident[:, :])
                done(ins)
            assert n[0] == PRE_PE, n[0]
            pe.wait_ge(pre_dve, PRE_DVE)
            pe.wait_ge(pre_act, PRE_ACT)

            def turn(q, k, r, it):
                pe.wait_ge(ld_hist[k][r], 16 * (it + 1))
                for ab in range(2):
                    at_least(pe, hT_ready, 4 * q + 2 * r + ab - 1)
                    for c in range(C):
                        for t in range(NK):
                            ins = pe.transpose(bank[2 * ab + c][:, t * TR:(t + 1) * TR],
                                               hist[0:TR, k, (2 * r + ab) * NK + t, c * P:(c + 1) * P],
                                               ident[0:TR, 0:TR])
                    ins.then_inc(turned, 1)

            def first_layer(q, k, r):
                at_least(pe, qhT_ready, 4 * q + 2 * r + 2)
                if r == 0:
                    at_least(pe, din_masked, q)
                else:
                    at_least(pe, h2_sum, 2 * q)
                for i in range(2 * C):
                    x = (hT[:, k % 2, r], qhT[:, r])[i // C]
                    for ab in range(2):
                        ins = mm(bank[4 + r][ab * A:(ab + 1) * A, 0:GR], w1T[:, i, :],
                                 x[:, i % C, ab * GR:(ab + 1) * GR], i == 0, i == 2 * C - 1)
                ins.then_inc(layer1, 1)

            def second_layer(q, k, r):
                at_least(pe, h1_ready, 2 * q + r + 1)
                mm(bank[4 + r][:, 0:GR], w2T[:, :], h1[:, r, :]).then_inc(layer2, 1)

            def quad_logits(q, k):
                at_least(pe, quad_kq, q + 1)
                at_least(pe, log_masked, q)
                for c in range(C):
                    for g in range(4):
                        ins = mm(bank[6][32 * g:32 * g + 32, 0:GR], kq_quad[:, k % 2, c, 32 * g:32 * g + 32],
                                 hT[:, k % 2, g // 2, c, (g % 2) * GR:(g % 2 + 1) * GR], c == 0, c == C - 1)
                ins.then_inc(logits, 1)

            def quad_scores(q, k):
                at_least(pe, h2_ready, 2 * q + 2)
                for r in range(2):
                    ins = mm(bank[4][32 * r:32 * r + 32, 0:GR], w3_x[:, :], h2[:, r, :])
                ins.then_inc(scores, 1)

            def turn_logits(q):
                at_least(pe, log_probs, q + 1)
                at_least(pe, pooledT_ready, q)
                for t in range(NK):
                    ins = pe.transpose(bank[7][0:TR, t * P:(t + 1) * P], log_p[:, t * TR:(t + 1) * TR], ident[:, :])
                ins.then_inc(log_pT, 1)

            def turn_scores(q):
                pe.wait_ge(consts, 7)
                at_least(pe, din_probs, q + 1)
                at_least(pe, log_w, q + 1)
                for t in range(NK):
                    ins = pe.transpose(bank[7][0:TR, t * 64:(t + 1) * 64], din_p[:, t * TR:(t + 1) * TR],
                                       ident[0:64, 0:64])
                ins.then_inc(din_pT, 1)

            def pool_rows(q, k):
                at_least(pe, din_w, q + 1)
                for r in range(2):
                    for odd in range(2):
                        for c in range(NK):
                            t = r * (QT // 2) + 2 * c + odd
                            ins = mm(bank[7][32 * c:32 * c + 32, r * D:(r + 1) * D],
                                     p_w[0:TR, t, (16, 0)[odd]:(16, 0)[odd] + 32],
                                     hist[0:TR, k, t, :], odd == 0, odd == 1)
                ins.then_inc(pool_done, 1)

            def turn_pooled(q):
                at_least(pe, pooled_ready, q + 1)
                for c in range(C):
                    for r in range(2):
                        ins = pe.transpose(bank[7][:, (2 * c + r) * P:(2 * c + r + 1) * P],
                                           pooled[:, r, c * P:(c + 1) * P], ident[:, :])
                ins.then_inc(pooledT, 1)

            def step(q, k, it=0, last=False):
                one, two = (k - 1) % RING, (k - 2) % RING
                here = lambda back: not isinstance(q, int) or 0 <= q - back < NQ
                if here(0):
                    turn(q, k, 0, it)
                if here(1):
                    first_layer(q - 1, one, 1)
                if here(2):
                    turn_scores(q - 2)
                if here(1):
                    second_layer(q - 1, one, 0)
                    quad_logits(q - 1, one)
                    second_layer(q - 1, one, 1)
                if here(2):
                    pool_rows(q - 2, two)
                if here(1):
                    quad_scores(q - 1, one)
                if here(2):
                    turn_pooled(q - 2)
                if here(0):
                    turn(q, k, 1, it)
                    first_layer(q, k, 0)
                if here(1):
                    turn_logits(q - 1)

            for k in range(RING):
                step(k, k)
            with pe.Fori(1, NQ // RING) as it:
                for k in range(RING):
                    step(it * RING + k, k, it)
            step(NQ, 0)
            step(NQ + 1, 1)

            pe.wait_ge(pooledT_ready, NQ)
            for et in range(2):
                for c in range(C):
                    for h in (2 * et, 2 * et + 1):
                        ins = mm(bank[et][(h % 2) * HD:(h % 2 + 1) * HD, :], wvT[:, c, h * HD:(h + 1) * HD],
                                 view(headT, c * B * H + h, [(H, B)]), c == 0, c == C - 1)
                ins.then_inc(v_done, 1)
            for o in range(C):
                for et in range(C):
                    pe.wait_ge(v_ready, et + 1)
                    ins = mm(bank[2 + o][:, :], outwT[:, et, o * P:(o + 1) * P], vT[:, et, :], et == 0, et == C - 1)
                ins.then_inc(mha_done, 1)
            for j in range(BB):
                for c in range(C):
                    mm(bank[4 + j][:, 0:D], interestT[:, c, j * P:(j + 1) * P], woT[:, c, :], c == 0, False)
            pe.wait_ge(mha_ready, C)
            for j in range(BB):
                for c in range(C):
                    ins = mm(bank[4 + j][:, 0:D], mhaT[:, c, j * P:(j + 1) * P], woT[:, C + c, :], False, c == C - 1)
                ins.then_inc(z_done, 1)

        @block.scalar
        def _(act):
            n = [0]

            def done(ins):
                n[0] += 1
                ins.then_inc(pre_act, 1)

            cols = lambda t: t.rearrange("(n p) -> p n", p=P)
            act.wait_ge(prepared, 1)
            for r in range(2):
                act.dma_start(w2_n[r * A:(r + 1) * A, r * A:(r + 1) * A], W2).then_inc(ld_w2, 16)
            act.dma_start(mask_i[:, :, :], mask.rearrange("(q b) s -> b q s", b=QB)).then_inc(ld_mask, 16)
            for r in range(2):
                act.dma_start(b1_c[r * A:(r + 1) * A, :], b1.unsqueeze(1)).then_inc(ld_small, 16)
                act.dma_start(b2_c[r * A:(r + 1) * A, :], b2.unsqueeze(1)).then_inc(ld_small, 16)
                act.dma_start(w3_c[r * A:(r + 1) * A, :], W3.rearrange("o a -> a o"), allow_slow_non_contiguous=True).then_inc(ld_small, 16)
            act.dma_start(inb_c[:, :], cols(in_b), allow_slow_non_contiguous=True).then_inc(ld_small, 16)
            act.dma_start(b3_c[:, :], b3.unsqueeze(0).to_broadcast([64, 1])).then_inc(ld_small, 16)
            act.dma_start(a1_c[:, :], a1.unsqueeze(0).to_broadcast([P, 1])).then_inc(ld_small, 16)
            act.dma_start(a2_c[:, :], a2.unsqueeze(0).to_broadcast([P, 1])).then_inc(ld_small, 16)
            act.dma_start(outb_c[:, :], cols(out_b), allow_slow_non_contiguous=True).then_inc(ld_late, 16)
            act.dma_start(ao_c[:, :], ao.unsqueeze(0).to_broadcast([P, 1])).then_inc(ld_late, 16)
            act.dma_start(bo_b[:, :], bo.unsqueeze(0).to_broadcast([P, D])).then_inc(ld_late, 16)
            act.dma_start(lnw_b[:, :], ln_w.unsqueeze(0).to_broadcast([P, D])).then_inc(ld_late, 16)
            act.dma_start(lnb_b[:, :], ln_b.unsqueeze(0).to_broadcast([P, D])).then_inc(ld_late, 16)
            for c in range(C):
                act.wait_ge(pre_pe, 1 + c)
                done(act.copy(qT[:, c, :], bank[c][:, :]))
            act.wait_ge(pre_pe, 3)
            done(act.copy(wqT[:, :, :].rearrange("p c e -> p (c e)"), bank[2][:, :]))
            for i in range(H * C):
                act.wait_ge(pre_pe, 10 + i)
                h, c = i // C, i % C
                done(act.copy(view(kq, c * B * H + h, [(H, B)]), bank[1 + i % 2][:, :]))
            act.wait_ge(pre_dve, 13)
            for h in range(H):
                to = qbk[h:h + 1, :]
                act.dma_start(bass.AP(to.tensor, to.offset, [[H * NQ, QB], [1, NQ]]),
                              qbk_r[h:h + 1, :, :]).then_inc(qbk_moved, 16)
            for i, (dst, src) in enumerate(((wvT[:, :, :], bank[7]), (outwT[:, :, :], bank[1]),
                                            (woT[:, 0:C, :], bank[2]), (woT[:, C:2 * C, :], bank[0]))):
                act.wait_ge(pre_pe, 22 + i)
                done(act.copy(dst.rearrange("p c e -> p (c e)"), src[:, :]))
            assert n[0] == PRE_ACT, n[0]

            def take_turned(q, k, r):
                for ab in range(2):
                    at_least(act, turned, 4 * q + 2 * r + ab + 1)
                    act.copy(view(hT, (((k % 2) * 2 + r) * C) * 2 * GR + ab * GR, [(2 * GR, C), (1, GR)]),
                             psum[:, 2 * ab:2 * ab + 2, 0:GR]).then_inc(hT_ready, 1)

            def add_b2(q, r):
                at_least(act, layer2, 2 * q + r + 1)
                act.activation(h2[:, r, :], bank[4 + r][:, 0:GR], ACT.Identity, bias=b2_s[:, :]).then_inc(h2_sum, 1)

            def exp_logits(q):
                at_least(act, log_masked, q + 1)
                act.activation(log_p[:, :], log_t[:, :], ACT.Exp, bias=small[:, 0:1], scale=-1.0,
                               accum_out=small[:, 1:2]).then_inc(log_exp, 1)

            def exp_scores(q):
                at_least(act, din_masked, q + 1)
                act.activation(din_p[:, :], din_t[:, :], ACT.Exp, bias=small[0:64, 2:3], scale=-1.0,
                               accum_out=small[0:64, 3:4]).then_inc(din_exp, 1)

            def take_pooled(q):
                at_least(act, pool_done, q + 1)
                act.copy(pooled[:, :, :].rearrange("p r d -> p (r d)"), bank[7][:, :]).then_inc(pooled_ready, 1)

            def step(q, k):
                here = lambda back: not isinstance(q, int) or 0 <= q - back < NQ
                if here(0):
                    take_turned(q, k, 0)
                if here(1):
                    add_b2(q - 1, 0)
                    add_b2(q - 1, 1)
                    exp_logits(q - 1)
                if here(2):
                    take_pooled(q - 2)
                if here(0):
                    take_turned(q, k, 1)
                if here(1):
                    exp_scores(q - 1)

            for k in range(RING):
                step(k, k)
            with act.Fori(1, NQ // RING) as it:
                for k in range(RING):
                    step(it * RING + k, k)
            step(NQ, 0)
            step(NQ + 1, 1)

            for et in range(C):
                act.wait_ge(v_done, et + 1)
                act.activation(vT[:, et, :], bank[et][:, :], ACT.Identity,
                               bias=inb_c[:, 2 * C + et:2 * C + et + 1]).then_inc(v_ready, 1)
            for o in range(C):
                act.wait_ge(mha_done, o + 1)
                act.activation(mhaT[:, o, :], bank[2 + o][:, :], ACT.Identity,
                               bias=outb_c[:, o:o + 1]).then_inc(mha_ready, 1)

        @block.vector
        def _(dve):
            n = [0]

            def done(ins):
                n[0] += 1
                ins.then_inc(pre_dve, 1)

            dve.memset(w2_n[:, :], 0.0).then_inc(prepared, 1)
            dve.memset(q_x[:, :, :, :], 0.0)
            dve.memset(bk_x[:, :, :], 0.0)
            dve.memset(w3_x[:, :], 0.0)
            dve.memset(p_w[:, :, :], 0.0)
            dve.wait_ge(ld_w1, 16)
            dve.tensor_tensor(w1_c[:, 0, :], w1_n[:, 0, :], w1_n[:, 2, :], ALU.add)
            dve.tensor_tensor(w1_c[:, 1, :], w1_n[:, 1, :], w1_n[:, 2, :], ALU.subtract).then_inc(prepared, 1)
            dve.wait_ge(ld_small, 16 * N_SMALL)
            for i, a in enumerate((a1_c, a2_c)):
                dve.tensor_scalar(sign[:, i:i + 1], a[:, :], 1.0, 2.0, ALU.is_le, ALU.mult).then_inc(signs, 1)
            dve.wait_ge(signs, 2)
            dve.tensor_scalar(sign[:, 3:5], sign[:, 0:2], -1.0, None, ALU.add).then_inc(signs, 1)
            dve.wait_ge(signs, 3)
            sign1, sign2 = sign[:, 3:4], sign[:, 4:5]
            dve.tensor_tensor(sign[:, 5:6], sign1, sign2, ALU.mult).then_inc(signs, 1)
            dve.tensor_tensor(b1_s[:, :], b1_c[:, :], sign1, ALU.mult).then_inc(signs, 1)
            dve.tensor_tensor(b2_s[:, :], b2_c[:, :], sign2, ALU.mult).then_inc(signs, 1)
            dve.wait_ge(signs, 6)
            dve.wait_ge(pre_pe, 4)
            done(dve.tensor_scalar(w1T[:, :, :].rearrange("p i a -> p (i a)"), bank[3][:, 0:4 * A], sign1, None,
                                   ALU.mult))
            for i in range(2):
                done(dve.tensor_scalar(w1uT[:, :, i, :], bank[3][:, 4 * A:6 * A].rearrange("p (c a) -> p c a", a=A),
                                       sign1, None, ALU.mult))
            dve.wait_ge(pre_pe, 5)
            done(dve.tensor_scalar(w2T[:, :], bank[4][:, 0:P], sign[:, 5:6], None, ALU.mult))
            for r in range(2):
                dve.tensor_scalar(w3_x[r * A:(r + 1) * A, 16 * r:16 * r + GB],
                                  w3_c[r * A:(r + 1) * A, :].to_broadcast([A, GB]),
                                  sign[r * A:(r + 1) * A, 4:5], None, ALU.mult)
            for h in range(H):
                r = h % 2
                ins = dve.tensor_copy(bk_x[r * HD:(r + 1) * HD, h // 2, h:h + 1],
                                      inb_c[r * HD:(r + 1) * HD, C + h // 2:C + h // 2 + 1])
            done(ins)
            for t in range(C):
                dve.wait_ge(pre_pe, 6 + t)
                done(dve.tensor_scalar(q_e[:, t, :], bank[5 + t][:, :], inb_c[:, t:t + 1], None, ALU.add))
                for r in range(2):
                    ins = dve.tensor_scalar(q_x[r * HD:(r + 1) * HD, r, t, :], bank[5 + t][r * HD:(r + 1) * HD, :],
                                            inb_c[r * HD:(r + 1) * HD, t:t + 1], None, ALU.add)
                done(ins)
            dve.wait_ge(ld_mask, 16)
            done(dve.tensor_scalar(mask_f[:, :, :], mask_i[:, :, :], 0.0, -1.0, ALU.not_equal, ALU.add))
            dve.wait_ge(pre_pe, 8)
            for r in range(2):
                src = bank[7][r * A:(r + 1) * A, :].rearrange("p (n g e) -> p n g e", g=2, e=GB)[:, :, r, :]
                done(dve.tensor_scalar(u[r * A:(r + 1) * A, :, :], src, b1_s[r * A:(r + 1) * A, :], None, ALU.add))
            dve.wait_ge(pre_pe, 9)
            done(dve.tensor_copy(qbk_r[:, :, :], bank[0][0:H, :].rearrange("h (q b) -> h b q", b=QB)))
            half = NQ // 2
            dve.wait_ge(qbk_moved, 16 * H)
            for i in range(2):
                dve.wait_ge(pre_pe, 18 + i)
                done(dve.scalar_tensor_tensor(
                    own_log[:, i * half:(i + 1) * half, :],
                    bank[3 + i][:, 0:half * S].rearrange("p (q s) -> p q s", s=S), BIG,
                    qbk[:, i * half:(i + 1) * half].unsqueeze(2).to_broadcast([P, half, S]), ALU.mult, ALU.add))
            for i in range(2):
                dve.wait_ge(pre_pe, 20 + i)
                done(dve.tensor_scalar(own_din[:, i * half:(i + 1) * half, :],
                                       bank[5 + i][0:64, 0:half * S].rearrange("p (q s) -> p q s", s=S), BIG,
                                       b3_c[:, :], ALU.mult, ALU.add))
            for m, src in ((other_log[:, :], bank[3][:, half * S:half * S + GB]),
                           (other_din[:, :], bank[5][0:64, half * S:half * S + GB])):
                done(dve.tensor_scalar(m, src, -1.0, BIG, ALU.add, ALU.mult))
            assert n[0] == PRE_DVE, n[0]

            def times_query(q, k, r):
                for ab in range(2):
                    g = 4 * q + 2 * r + ab
                    at_least(dve, hT_ready, g + 1)
                    off, dims = r * C * 2 * GR + ab * GR, [(2 * GR, C), (S, GB), (1, S)]
                    dve.tensor_tensor(view(qhT, off, dims), view(hT, (k % 2) * 2 * C * 2 * GR + off, dims),
                                      qT[:, :, bass.ds(g * GB, GB)].unsqueeze(3).to_broadcast([P, C, GB, S]),
                                      ALU.mult).then_inc(qhT_ready, 1)

            def add_query(q, r):
                at_least(dve, layer1, 2 * q + r + 1)
                dve.tensor_tensor(h1[:, r, :].rearrange("p (e s) -> p e s", s=S),
                                  bank[4 + r][:, 0:GR].rearrange("p (e s) -> p e s", s=S),
                                  u[:, bass.ds(2 * q + r, 1), :].rearrange("p n e -> p (n e)").unsqueeze(2)
                                  .to_broadcast([P, GB, S]), ALU.add).then_inc(h1_sum, 1)

            def prelu1(q, r):
                at_least(dve, h1_sum, 2 * q + r + 1)
                dve.scalar_tensor_tensor(h1[:, r, :], h1[:, r, :], a1_c[:, :], h1[:, r, :], ALU.mult,
                                         ALU.max).then_inc(h1_ready, 1)

            def prelu2(q, r):
                at_least(dve, h2_sum, 2 * q + r + 1)
                dve.scalar_tensor_tensor(h2[:, r, :], h2[:, r, :], a2_c[:, :], h2[:, r, :], ALU.mult,
                                         ALU.max).then_inc(h2_ready, 1)

            def mask_logits(q, k):
                dve.wait_ge(qbk_moved, 16 * H)
                at_least(dve, logits, q + 1)
                at_least(dve, quad_masks, 2 * q + 2)
                dve.tensor_tensor_reduce(log_t[:, :], bank[6][:, 0:GR], mask_log[:, k % 2, :],
                                         -1.0 / HD ** 0.5, 3e38, ALU.add, ALU.min,
                                         small[:, 0:1]).then_inc(log_masked, 1)

            def mask_scores(q, k):
                dve.wait_ge(qbk_moved, 16 * H)
                at_least(dve, scores, q + 1)
                at_least(dve, quad_masks, 2 * q + 2)
                dve.tensor_tensor_reduce(din_t[:, :], bank[4][0:64, 0:GR], mask_din[:, k % 2, :], -1.0, 3e38,
                                         ALU.add, ALU.min, small[0:64, 2:3]).then_inc(din_masked, 1)

            def normalise_logits(q):
                at_least(dve, log_exp, q + 1)
                dve.reciprocal(small[:, 4:5], small[:, 1:2]).then_inc(recips, 1)
                at_least(dve, recips, 2 * q + 1)
                dve.tensor_scalar(log_p[:, :], log_p[:, :], small[:, 4:5], None, ALU.mult).then_inc(log_probs, 1)

            def normalise_scores(q):
                at_least(dve, din_exp, q + 1)
                dve.reciprocal(small[0:64, 5:6], small[0:64, 3:4]).then_inc(recips, 1)
                at_least(dve, recips, 2 * q + 2)
                dve.tensor_scalar(din_p[:, :], din_p[:, :], small[0:64, 5:6], None, ALU.mult).then_inc(din_probs, 1)

            def place_logits(q):
                at_least(dve, log_pT, q + 1)
                dve.tensor_copy(view(p_w, 16, [(NK * PW, 4), (PW, NK), (1, 8)], TR),
                                view(psum, 7 * 512, [(32, 4), (P + 8, NK), (1, 8)], TR)).then_inc(log_w, 1)

            def place_scores(q):
                at_least(dve, din_pT, q + 1)
                dve.tensor_copy(view(p_w, 24, [(NK * PW, 4), (PW, NK), (1, 2)], TR),
                                view(psum, 7 * 512, [(16, 4), (64 + 2, NK), (1, 2)], TR)).then_inc(din_w, 1)

            def take_pooledT(q):
                at_least(dve, pooledT, q + 1)
                src = bank[7][:, :].rearrange("p (c t x) -> p c t x", c=C, x=16)
                dve.tensor_copy(headT[:, :, bass.ds(q * P, P)].rearrange("p c (t x) -> p c t x", x=8),
                                src[:, :, :, 0:8])
                dve.tensor_copy(interestT[:, :, bass.ds(q * QB, QB)].rearrange("p c (t x) -> p c t x", x=2),
                                src[:, :, :, 8:10]).then_inc(pooledT_ready, 1)

            def step(q, k):
                one = (k - 1) % RING
                here = lambda back: not isinstance(q, int) or 0 <= q - back < NQ
                if here(0):
                    times_query(q, k, 0)
                if here(1):
                    add_query(q - 1, 1)
                if here(2):
                    place_scores(q - 2)
                if here(1):
                    prelu1(q - 1, 1)
                    prelu2(q - 1, 0)
                    mask_logits(q - 1, one)
                    prelu2(q - 1, 1)
                    normalise_logits(q - 1)
                    mask_scores(q - 1, one)
                if here(2):
                    take_pooledT(q - 2)
                if here(0):
                    times_query(q, k, 1)
                if here(1):
                    normalise_scores(q - 1)
                if here(0):
                    add_query(q, 0)
                if here(1):
                    place_logits(q - 1)
                if here(0):
                    prelu1(q, 0)

            for k in range(RING):
                step(k, k)
            with dve.Fori(1, NQ // RING) as it:
                for k in range(RING):
                    step(it * RING + k, k)
            step(NQ, 0)
            step(NQ + 1, 1)

            for j in range(BB):
                dve.wait_ge(z_done, j + 1)
                dve.tensor_tensor(z[:, j, :], bank[4 + j][:, 0:D], bo_b[:, :], ALU.add).then_inc(z_ready, 1)
                dve.wait_ge(z_ready, j + 1)
                dve.bn_stats(stats[:, j, :], z[:, j, :]).then_inc(z_stats, 1)
                dve.wait_ge(z_stats, j + 1)
                dve.bn_aggr(moments[:, j, :], stats[:, j, :]).then_inc(z_moments, 1)
                dve.wait_ge(z_moments, 2 * j + 1)
                dve.tensor_scalar(rstd[:, j, 0:1], moments[:, j, 1:2], EPS, None, ALU.add).then_inc(z_moments, 1)
            for j in range(BB):
                dve.wait_ge(z_rstd, j + 1)
                dve.tensor_scalar(zn[:, j, :], z[:, j, :], moments[:, j, 0:1], rstd[:, j, 1:2],
                                  ALU.subtract, ALU.mult).then_inc(z_norm, 1)
                dve.wait_ge(z_norm, j + 1)
                dve.tensor_tensor(zn[:, j, :], zn[:, j, :], lnw_b[:, :], ALU.mult).then_inc(z_scaled, 1)
                dve.wait_ge(z_scaled, j + 1)
                dve.tensor_tensor(zn[:, j, :], zn[:, j, :], lnb_b[:, :], ALU.add).then_inc(z_shifted, 1)
                dve.wait_ge(z_shifted, j + 1)
                dve.tensor_scalar(z[:, j, :], zn[:, j, :], 0.0, ao_c[:, :], ALU.min, ALU.mult).then_inc(z_below, 1)
                dve.wait_ge(z_below, j + 1)
                dve.scalar_tensor_tensor(z[:, j, :], zn[:, j, :], 0.0, z[:, j, :], ALU.max, ALU.add).then_inc(y_ready, 1)


_INS = ['r_history_mask', 'L0_rec_query', 'L0_rec_history', 'L0_rec_W1', 'L0_rec_b1', 'L0_rec_a1', 'L0_rec_W2',
        'L0_rec_b2', 'L0_rec_a2', 'L0_rec_W3', 'L0_rec_b3', 'L0_rec_in_w', 'L0_rec_in_b', 'L0_rec_out_w',
        'L0_rec_out_b', 'L0_rec_Wo', 'L0_rec_bo', 'L0_rec_ln_w', 'L0_rec_ln_b', 'L0_rec_ao']


def kernel(**inputs):
    import numpy as _np
    import concourse.bacc as _bacc
    from concourse import mybir as _mybir
    from concourse.bass_utils import run_bass_kernel_spmd as _run

    nc = _bacc.Bacc("TRN2", target_bir_lowering=False, num_devices=1)
    arrays, args = {}, []
    for name in _INS:
        a = _np.ascontiguousarray(inputs[name])
        a = a.reshape(a.shape or (1,))
        arrays[f"in_{name}_dram"] = a
        args.append(nc.dram_tensor(f"in_{name}_dram", a.shape, _mybir.dt.from_np(a.dtype), kind="ExternalInput").ap())
    shape = inputs['L0_rec_query'].shape
    args.append(nc.dram_tensor("out_0_dram", shape, F32, kind="ExternalOutput").ap())
    rec_kernel(nc, *args)
    r = _run(nc, [arrays], core_ids=[0])
    return r.results[0]["out_0_dram"]
```

```python
from contextlib import ExitStack

import concourse.bass as bass
from concourse import mybir

F32 = mybir.dt.float32
BF16 = mybir.dt.bfloat16
I32 = mybir.dt.int32
ALU = mybir.AluOpType
ACT = mybir.ActivationFunctionType

BIG = 1e30
EPS = 1e-5


def at_least(engine, semaphore, count):
    if isinstance(count, int) and count <= 0:
        return
    engine.wait_ge(semaphore, count)


def rec_kernel(nc, mask, query, history, W1, b1, a1, W2, b2, a2, W3, b3, in_w, in_b, out_w, out_b,
               Wo, bo, ln_w, ln_b, ao, out):
    B, S, D = history.shape
    A = W2.shape[0]
    H = 4
    HD = D // H
    P = 128
    C = D // P
    GB = 8
    GR = GB * S
    TR = 2 * S
    NK = GR // TR
    QB = 4 * GB
    QT = 4 * NK
    NQ = B // QB
    RING = 4
    BB = B // P
    SIDE = GB // 2 * S
    PW = 48
    WARM_UP = 14
    assert (C, A, HD, TR, NQ % RING, RING * QB) == (2, 64, 64, 100, 0, P)

    hist_v = history.rearrange("(q r t e) s d -> q r (e s) t d", r=2, t=QT // 2, e=2)

    with ExitStack() as ctx:
        def sb(name, shape, dt=F32):
            return ctx.enter_context(nc.sbuf_tensor(name, shape, dt))

        def sem(name):
            return ctx.enter_context(nc.semaphore(name))

        hist = sb("hist", [P, RING, QT, D])
        hT = sb("hT", [P, 2, 2, C, 2 * GR])
        qhT = sb("qhT", [P, 2, C, 2 * GR])
        h1 = sb("h1", [P, 2, GR])
        h2 = sb("h2", [P, 2, GR])
        log_t = sb("log_t", [P, GR])
        log_p = sb("log_p", [P, GR])
        din_t = sb("din_t", [P, SIDE])
        din_p = sb("din_p", [P, SIDE])
        small = sb("small", [P, 8])
        p_w = sb("p_w", [P, QT, PW])
        pooled = sb("pooled", [P, 2, D])
        headT = sb("headT", [P, C, P * H])
        interestT = sb("interestT", [P, C, P])
        kq = sb("kq", [P, C, B * H])
        kq_quad = sb("kq_quad", [P, 2, C, P])
        mask_log = sb("mask_log", [P, 2, GR])
        mask_din = sb("mask_din", [P, 2, SIDE])
        own_log = sb("own_log", [P, NQ, S])
        own_din = sb("own_din", [P, NQ, S])
        other_log = sb("other_log", [P, GB])
        other_din = sb("other_din", [P, GB // 2])
        ident = sb("ident", [P, P])
        mask_i = sb("mask_i", [QB, NQ, S], I32)
        mask_b = sb("mask_b", [QB, NQ, S], BF16)
        to_log = sb("to_log", [QB, GB // 2, GB, H], BF16)
        to_din = sb("to_din", [QB, GB, 16], BF16)
        of_group = sb("of_group", [QB, GB], BF16)
        of_side = sb("of_side", [QB, GB // 2], BF16)
        query_n = hist[:, RING - 1, 0:4, :]
        inw_n = hist[:, RING - 1, 4:10, :]
        outw_n = hist[:, RING - 1, 10:12, :]
        wo_n = hist[:, RING - 1, 12:16, :].rearrange("p (t x) d -> p t (x d)", t=C)
        qT = sb("qT", [P, C, B])
        w1_n = sb("w1_n", [A, 4, D])
        w1_c = sb("w1_c", [A, 2, D])
        w1T = sb("w1T", [P, 2 * C, A])
        w1uT = sb("w1uT", [P, C, A])
        u = sb("u", [P, 2 * NQ, GB])
        b1_c = sb("b1_c", [P, 1])
        b2_c = sb("b2_c", [P, 1])
        b3_c = sb("b3_c", [P, 1])
        a1_c = sb("a1_c", [P, 1])
        a2_c = sb("a2_c", [P, 1])
        ao_c = sb("ao_c", [P, 1])
        sign = sb("sign", [P, 8])
        b1_s = sb("b1_s", [P, 1])
        b2_s = sb("b2_s", [P, 1])
        w2_n = sb("w2_n", [A, 2, A])
        w2T = sb("w2T", [P, P])
        w3_c = sb("w3_c", [P, 1])
        w3_x = sb("w3_x", [P, 32])
        inb_c = sb("inb_c", [P, 3 * C])
        bk_x = sb("bk_x", [P, C, H])
        wqT = sb("wqT", [P, C, D])
        wvT = sb("wvT", [P, C, D])
        early = hT[:, 1, :, :, :].rearrange("p r c n -> p (r c n)")
        q_x = early[:, 0:2 * C * B].rearrange("p (r c b) -> p r c b", r=2, c=C)
        q_e = early[:, 2 * C * B:3 * C * B].rearrange("p (c b) -> p c b", c=C)
        qbk_r = sb("qbk_r", [H, QB, NQ])
        qbk = sb("qbk", [P, NQ])
        outb_c = sb("outb_c", [P, C])
        outb_x = sb("outb_x", [P, C, P])
        woT = sb("woT", [P, 2 * C, D])
        w_mix = sb("w_mix", [P, C, D])
        bo_b = sb("bo_b", [P, D])
        b_mix = sb("b_mix", [P, D])
        lnw_b = sb("lnw_b", [P, D])
        lnb_b = sb("lnb_b", [P, D])
        vT = sb("vT", [P, C, P])
        interest_k = sb("interest_k", [P, C, P])
        z = sb("z", [P, D])
        zn = sb("zn", [P, D])
        y = sb("y", [P, D])
        stats = sb("stats", [P, 6])
        moments = sb("moments", [P, 2])
        rstd = sb("rstd", [P, 2])
        minus_half = sb("minus_half", [P, 1])

        psum = ctx.enter_context(nc.psum_tensor("psum", [P, 8, 512], F32))
        bank = [psum[:, i, :] for i in range(8)]

        def view(t, offset, dims, parts=P, start=0):
            base = t[start:start + parts]
            free = 1
            for n in t.shape[1:]:
                free *= n
            return bass.AP(base.tensor, base.offset + offset, [[free, parts]] + [list(d) for d in dims])

        ld_query, ld_w1, ld_wq, ld_wk, ld_w2 = (
            sem("ld_query"), sem("ld_w1"), sem("ld_wq"), sem("ld_wk"), sem("ld_w2"))
        ld_late, ld_mask, ld_prelu, ld_bias, ld_small, ld_rows = (
            sem("ld_late"), sem("ld_mask"), sem("ld_prelu"), sem("ld_bias"), sem("ld_small"), sem("ld_rows"))
        ld_hist = [[sem(f"ld_hist{k}{r}") for r in range(2)] for k in range(RING)]
        consts, cleared, prepared = sem("consts"), sem("cleared"), sem("prepared")
        cleared_v = sem("cleared_v")
        query_turned, w1_turned, u_done, wq_turned, w2_turned, q_done, own_done, wv_turned, wo_turned = (
            sem("query_turned"), sem("w1_turned"), sem("u_done"), sem("wq_turned"), sem("w2_turned"),
            sem("q_done"), sem("own_done"), sem("wv_turned"), sem("wo_turned"))
        qbk_done, kq_done, mix_done, b_mix_done = sem("qbk_done"), sem("kq_done"), sem("mix_done"), sem("b_mix_done")
        query_kept, wq_kept, wv_kept, wo_kept, kq_kept, mix_kept = (
            sem("query_kept"), sem("wq_kept"), sem("wv_kept"), sem("wo_kept"), sem("kq_kept"), sem("mix_kept"))
        q_kept = sem("q_kept")
        w1T_ready, u_ready, w2T_ready, bk_ready, mask_ready, q_ready, qbk_rows, own_ready, outb_ready, b_mix_ready = (
            sem("w1T_ready"), sem("u_ready"), sem("w2T_ready"), sem("bk_ready"), sem("mask_ready"), sem("q_ready"),
            sem("qbk_rows"), sem("own_ready"), sem("outb_ready"), sem("b_mix_ready"))
        qbk_moved, last_stored = sem("qbk_moved"), sem("last_stored")
        turned = sem("turned")
        hT_ready = sem("hT_ready")
        qhT_ready = sem("qhT_ready")
        layer1 = sem("layer1")
        h1_sum = sem("h1_sum")
        h1_ready = sem("h1_ready")
        layer2 = sem("layer2")
        h2_sum = sem("h2_sum")
        h2_ready = sem("h2_ready")
        signs = sem("signs")
        logits = sem("logits")
        scores = sem("scores")
        log_masked, din_masked = sem("log_masked"), sem("din_masked")
        log_exp, din_exp = sem("log_exp"), sem("din_exp")
        log_probs, din_probs = sem("log_probs"), sem("din_probs")
        recips = sem("recips")
        log_pT, din_pT = sem("log_pT"), sem("din_pT")
        log_w, din_w = sem("log_w"), sem("din_w")
        pool_done = sem("pool_done")
        pooled_ready = sem("pooled_ready")
        pooledT = sem("pooledT")
        pooledT_ready = sem("pooledT_ready")
        quad_kq = sem("quad_kq")
        quad_masks = sem("quad_masks")
        v_done, v_ready, interest_kept = sem("v_done"), sem("v_ready"), sem("interest_kept")
        z_done, z_ready, z_stats, z_moments = sem("z_done"), sem("z_ready"), sem("z_stats"), sem("z_moments")
        z_eps, z_rstd, z_norm, z_scaled, z_shifted = (
            sem("z_eps"), sem("z_rstd"), sem("z_norm"), sem("z_scaled"), sem("z_shifted"))
        z_below, z_above, y_ready, stored = sem("z_below"), sem("z_above"), sem("y_ready"), sem("stored")

        block = ctx.enter_context(nc.Block())

        def softmax_bank(q):
            return 1 if isinstance(q, int) and q == NQ - 1 else 7

        @block.sync
        def _(sp):
            def load(q, k, r):
                at_least(sp, pool_done, q - RING + 1)
                sp.dma_start(hist[0:TR, k, r * (QT // 2):(r + 1) * (QT // 2), :],
                             hist_v[q, r]).then_inc(ld_hist[k][r], 16)

            def load_weight(dst, src, t0, t1, signal):
                sp.dma_start(dst, src.rearrange("(t p) d -> p t d", p=P)[:, t0:t1, :]).then_inc(signal, 16)

            sp.dma_start(query_n, query.rearrange("(j p) d -> p j d", p=P)).then_inc(ld_query, 16)
            sp.dma_start(w1_n[:, :, :], W1.rearrange("a (f d) -> a f d", f=4)).then_inc(ld_w1, 16)
            load(0, 0, 0)
            load_weight(inw_n[:, 0:C, :], in_w, 0, C, ld_wq)
            sp.dma_start(w2_n[:, :, :], W2.unsqueeze(1).to_broadcast([A, 2, A])).then_inc(ld_w2, 16)
            load(0, 0, 1)
            load_weight(inw_n[:, C:2 * C, :], in_w, C, 2 * C, ld_wk)
            load_weight(inw_n[:, 2 * C:3 * C, :], in_w, 2 * C, 3 * C, ld_late)
            load_weight(wo_n[:, :, :], Wo, 0, C, ld_late)
            load_weight(outw_n[:, :, :], out_w, 0, C, ld_late)
            for k in range(1, RING - 1):
                for r in range(2):
                    load(k, k, r)
            sp.wait_ge(qbk_rows, 1)
            for h in range(H):
                to = qbk[h:h + 1, :]
                sp.dma_start(bass.AP(to.tensor, to.offset, [[H * NQ, QB], [1, NQ]]),
                             qbk_r[h:h + 1, :, :]).then_inc(qbk_moved, 16)
            sp.wait_ge(mix_done, 1)
            for r in range(2):
                load(RING - 1, RING - 1, r)
            with sp.Fori(1, NQ // RING) as it:
                for k in range(RING):
                    for r in range(2):
                        load(it * RING + k, k, r)
            sp.wait_ge(y_ready, BB)
            sp.dma_start(out[(BB - 1) * P:BB * P, :], y[:, :]).then_inc(last_stored, 16)
            sp.wait_ge(stored, 16 * (BB - 1))
            sp.wait_ge(last_stored, 16)

        @block.gpsimd
        def _(pool):
            pool.memset(ident[:, :], 0.0).then_inc(cleared, 1)
            pool.wait_ge(cleared, 1)
            pool.affine_select(out=ident[:, :], in_=ident[:, :], compare_op=ALU.not_equal, fill=1.0, base=0,
                               pattern=[[-1, P]], channel_multiplier=1).then_inc(consts, 1)

            def cols(t):
                return t.rearrange("(n p) -> p n", p=P)

            pool.dma_start(mask_i[:, :, :], mask.rearrange("(q b) s -> b q s", b=QB)).then_inc(ld_mask, 16)
            pool.dma_start(inb_c[:, :], cols(in_b), allow_slow_non_contiguous=True).then_inc(ld_small, 16)
            pool.dma_start(w3_c[:, :], W3.rearrange("o a -> a o").unsqueeze(0).to_broadcast([2, A, 1]),
                           allow_slow_non_contiguous=True).then_inc(ld_small, 16)
            pool.dma_start(b3_c[:, :], b3.unsqueeze(0).to_broadcast([P, 1])).then_inc(ld_small, 16)
            pool.memset(to_log[:, :, :, :], 0.0).then_inc(cleared, 1)
            pool.memset(to_din[:, :, :], 0.0).then_inc(cleared, 1)
            pool.memset(of_group[:, :], 0.0).then_inc(cleared, 1)
            pool.memset(of_side[:, :], 0.0).then_inc(cleared, 1)
            pool.wait_ge(cleared, 5)
            pool.affine_select(out=to_log[:, :, :, :], in_=to_log[:, :, :, :], compare_op=ALU.not_equal, fill=1.0,
                               base=0, pattern=[[-GB, 4], [-1, GB], [0, H]], channel_multiplier=1).then_inc(consts, 1)
            pool.affine_select(out=to_din[:, :, 0:GB // 2], in_=to_din[:, :, 0:GB // 2], compare_op=ALU.not_equal,
                               fill=1.0, base=0, pattern=[[-GB // 2, GB], [-1, GB // 2]],
                               channel_multiplier=1).then_inc(consts, 1)
            for step_, sel in ((GB, of_group), (GB // 2, of_side)):
                for g in range(QB // step_):
                    pool.affine_select(out=sel[:, :], in_=sel[:, :], compare_op=ALU.not_equal, fill=1.0,
                                       base=-step_ * g, pattern=[[-1, step_]],
                                       channel_multiplier=1).then_inc(consts, 1)
                    pool.wait_ge(consts, 4 + g + (0 if sel is of_group else 4))
            pool.dma_start(outb_c[:, :], cols(out_b), allow_slow_non_contiguous=True).then_inc(ld_rows, 16)
            for row, src in ((ao_c, ao), (bo_b, bo), (lnw_b, ln_w), (lnb_b, ln_b)):
                pool.dma_start(row[:, :], src.unsqueeze(0).to_broadcast([P, src.shape[0]])).then_inc(ld_rows, 16)
            pool.memset(minus_half[:, :], -0.5).then_inc(z_eps, 1)

            def quad(q, k):
                at_least(pool, logits, q - 1)
                pool.tensor_copy(kq_quad[:, k % 2, :, :],
                                 kq[:, :, bass.ds(q * P, P)]).then_inc(quad_kq, 1)
                at_least(pool, log_masked, q - 1)
                at_least(pool, din_masked, q - 1)
                for m, own, other, n in ((mask_log, own_log, other_log, GB), (mask_din, own_din, other_din, GB // 2)):
                    pool.tensor_tensor(m[:, k % 2, :].rearrange("p (e s) -> p e s", s=S),
                                       other[:, :].unsqueeze(2).to_broadcast([P, n, S]),
                                       own[:, bass.ds(q, 1), :].to_broadcast([P, n, S]),
                                       ALU.add).then_inc(quad_masks, 1)

            def keep_interest(count):
                pool.wait_ge(z_eps, 1)
                at_least(pool, v_done, count)
                pool.tensor_copy(interest_k[:, :, :], interestT[:, :, :]).then_inc(interest_kept, 1)

            def inverse_deviation(count):
                at_least(pool, z_moments, 2 * count)
                pool.tensor_tensor(rstd[:, 1:2], rstd[:, 0:1], minus_half[:, :], ALU.pow).then_inc(z_rstd, 1)

            def finish_block(count):
                def long_met():
                    pool.wait_ge(z_eps, 1)

                long_met()
                at_least(pool, z_rstd, count)
                pool.tensor_scalar(zn[:, :], z[:, :], moments[:, 0:1], rstd[:, 1:2],
                                   ALU.subtract, ALU.mult).then_inc(z_norm, 1)
                at_least(pool, z_norm, count)
                pool.tensor_tensor(zn[:, :], zn[:, :], lnw_b[:, :], ALU.mult).then_inc(z_scaled, 1)
                at_least(pool, z_scaled, count)
                pool.tensor_tensor(zn[:, :], zn[:, :], lnb_b[:, :], ALU.add).then_inc(z_shifted, 1)
                long_met()
                at_least(pool, z_shifted, count)
                pool.tensor_scalar(y[:, :], zn[:, :], 0.0, ao_c[:, :], ALU.min, ALU.mult).then_inc(z_below, 1)
                long_met()
                at_least(pool, z_below, count)
                pool.tensor_scalar(zn[:, :], zn[:, :], 0.0, None, ALU.max).then_inc(z_above, 1)
                at_least(pool, z_above, count)
                pool.tensor_tensor(y[:, :], y[:, :], zn[:, :], ALU.add).then_inc(y_ready, 1)

            pool.wait_ge(kq_kept, H * C)
            pool.wait_ge(own_ready, 6)
            for k in range(RING):
                quad(k, k)
            pool.wait_ge(ld_rows, 16 * 5)
            pool.wait_ge(z_eps, 1)
            with pool.Fori(1, NQ // RING) as it:
                for k in range(RING - 1):
                    quad(it * RING + k, k)
                keep_interest(it)
                quad(it * RING + RING - 1, RING - 1)
                inverse_deviation(it)
                finish_block(it)
                at_least(pool, y_ready, it)
                pool.dma_start(out[bass.ds((it - 1) * P, P), :], y[:, :]).then_inc(stored, 16)
                pool.wait_ge(stored, 16 * it)
            inverse_deviation(BB)

        @block.tensor
        def _(pe):
            def mm(o, l, r, first=True, last=True):
                return pe.matmul(o, l, r, start=first, stop=last, skip_group_check=True)

            def turn_weight(dst, src, col0=0):
                for c in range(C):
                    for t in range(C):
                        ins = pe.transpose(dst[:, c * D + t * P:c * D + (t + 1) * P],
                                           src[:, t, col0 + c * P:col0 + (c + 1) * P], ident[:, :])
                return ins

            def start_layer1():
                pe.wait_ge(consts, 1)
                for _i in range(WARM_UP):
                    pe.transpose(bank[7][:, 0:P], ident[:, :], ident[:, :])
                pe.wait_ge(ld_query, 16)
                for c in range(C):
                    for j in range(BB):
                        ins = pe.transpose(bank[c][:, j * P:(j + 1) * P], query_n[:, j, c * P:(c + 1) * P],
                                           ident[:, :])
                    ins.then_inc(query_turned, 1)
                pe.wait_ge(prepared, 1)
                for i, src in enumerate((w1_c[:, 1, 0:P], w1_c[:, 1, P:D], w1_n[:, 3, 0:P], w1_n[:, 3, P:D],
                                         w1_c[:, 0, 0:P], w1_c[:, 0, P:D])):
                    ins = pe.transpose(bank[5][:, i * A:(i + 1) * A], src, ident[0:A, 0:A])
                ins.then_inc(w1_turned, 1)

            def query_part():
                pe.wait_ge(w1T_ready, 2)
                for c in range(C):
                    for ab in range(2):
                        ins = mm(bank[7][ab * A:(ab + 1) * A, 0:B // 2], w1uT[:, c, :],
                                 view(qT, c * B + ab * GB // 2, [(GB, B // GB), (1, GB // 2)]), c == 0, c == C - 1)
                ins.then_inc(u_done, 1)
                pe.wait_ge(ld_wq, 16)
                turn_weight(bank[6], inw_n).then_inc(wq_turned, 1)
                pe.wait_ge(ld_w2, 16)
                pe.transpose(bank[5][:, 0:A], w2_n[:, :, :].rearrange("p i a -> p (i a)"),
                             ident[0:A, 0:A]).then_inc(w2_turned, 1)

            def prepare_heads():
                pe.wait_ge(wq_kept, 1)
                pe.wait_ge(u_ready, 1)
                for t in range(C):
                    for c in range(C):
                        ins = mm(bank[6 + t][:, :], wqT[:, c, t * P:(t + 1) * P], qT[:, c, :], c == 0, c == C - 1)
                    ins.then_inc(q_done, 1)
                pe.wait_ge(consts, 15)
                pe.wait_ge(mask_ready, 1)
                pe.wait_ge(hT_ready, 4)
                half = NQ // 2
                log_l, din_l = (to_log[:, :, :, :].rearrange("b g e h -> b (g e h)"),
                                to_din[:, :, :].rearrange("b x e -> b (x e)"))
                mm(bank[0][:, half * S:half * S + GB], log_l, of_group[:, :])
                mm(bank[2][:, half * S:half * S + GB // 2], din_l, of_side[:, :])
                for i in range(4):
                    mm(bank[i][:, 0:half * S], (log_l, din_l)[i // 2],
                       mask_b[:, (i % 2) * half:(i % 2 + 1) * half, :].rearrange("b q s -> b (q s)")
                       ).then_inc(own_done, 1)
                pe.wait_ge(ld_late, 16 * 3)
                pe.wait_ge(w2T_ready, 1)
                turn_weight(bank[5], inw_n[:, 2 * C:3 * C, :]).then_inc(wv_turned, 1)
                pe.wait_ge(h1_sum, 1)
                turn_weight(bank[4], wo_n, D).then_inc(wo_turned, 1)
                pe.wait_ge(bk_ready, 1)
                pe.wait_ge(q_ready, C)
                for t in range(C):
                    ins = mm(bank[6][0:H, :], bk_x[:, t, :], q_e[:, t, :], t == 0, t == C - 1)
                ins.then_inc(qbk_done, 1)
                pe.wait_ge(ld_wk, 16)
                for h in range(H):
                    for c in range(C):
                        i = h * C + c
                        if i == 1:
                            pe.wait_ge(wv_kept, 1)
                        if i >= 2:
                            pe.wait_ge(kq_kept, i - 1)
                        if i == 4:
                            pe.wait_ge(qbk_rows, 1)
                            turn_weight(bank[6], wo_n).then_inc(wo_turned, 1)
                        mm(bank[(7, 5)[i % 2]][:, :], inw_n[:, C + h // 2, c * P:(c + 1) * P],
                           q_x[:, h % 2, h // 2, :]).then_inc(kq_done, 1)
                pe.wait_ge(wo_kept, 2)
                for et in range(C):
                    for c in range(C):
                        ins = mm(bank[4][:, et * D:(et + 1) * D], outw_n[:, c, et * P:(et + 1) * P],
                                 woT[:, C + c, :], c == 0, c == C - 1)
                ins.then_inc(mix_done, 1)
                pe.wait_ge(outb_ready, 1)
                for c in range(C):
                    ins = mm(bank[6][:, 0:D], outb_x[:, c, :], woT[:, C + c, :], c == 0, c == C - 1)
                ins.then_inc(b_mix_done, 1)

            def turn(q, k, r, it, groups=(0, 1)):
                if isinstance(q, int) and q == 0 and r == 0:
                    pe.wait_ge(query_kept, C)
                if isinstance(q, int) and q == 1 and r == 0:
                    pe.wait_ge(own_ready, 6)
                pe.wait_ge(ld_hist[k][r], 16 * (it + 1))
                for ab in groups:
                    at_least(pe, hT_ready, 4 * q + 2 * r + ab - 1)
                    for c in range(C):
                        for t in range(NK):
                            ins = pe.transpose(bank[2 * ab + c][:, t * TR:(t + 1) * TR],
                                               hist[0:TR, k, (2 * r + ab) * NK + t, c * P:(c + 1) * P],
                                               ident[0:TR, 0:TR])
                    ins.then_inc(turned, 1)

            def first_layer(q, k, r):
                at_least(pe, qhT_ready, 4 * q + 2 * r + 2)
                if r == 0:
                    at_least(pe, din_masked, q)
                else:
                    at_least(pe, h2_sum, 2 * q)
                for i in range(2 * C):
                    x = (hT[:, k % 2, r], qhT[:, r])[i // C]
                    sides = x[:, i % C, :].rearrange("p (h a n) -> p a h n", h=2, a=2)
                    for ab in range(2):
                        ins = mm(bank[4 + r][ab * A:(ab + 1) * A, 0:GR].rearrange("p (h n) -> p h n", h=2),
                                 w1T[:, i, :], sides[:, ab], i == 0, i == 2 * C - 1)
                ins.then_inc(layer1, 1)

            def second_layer(q, k, r):
                at_least(pe, h1_ready, 2 * q + r + 1)
                mm(bank[4 + r][:, 0:GR], w2T[:, :], h1[:, r, :]).then_inc(layer2, 1)

            def quad_logits(q, k):
                at_least(pe, quad_kq, q + 1)
                at_least(pe, log_masked, q)
                for c in range(C):
                    for g in range(4):
                        ins = mm(bank[6][32 * g:32 * g + 32, 0:GR], kq_quad[:, k % 2, c, 32 * g:32 * g + 32],
                                 hT[:, k % 2, g // 2, c, (g % 2) * GR:(g % 2 + 1) * GR], c == 0, c == C - 1)
                ins.then_inc(logits, 1)

            def quad_scores(q, k):
                at_least(pe, h2_ready, 2 * q + 2)
                for r in range(2):
                    for half in range(2):
                        x = 2 * r + half
                        ins = mm(bank[4][32 * x:32 * x + 32, 0:SIDE], w3_x[:, :],
                                 h2[:, r, half * SIDE:(half + 1) * SIDE])
                ins.then_inc(scores, 1)

            def turn_logits(q, k, it):
                if k == 0:
                    at_least(pe, v_ready, it)
                if k == 1:
                    at_least(pe, z_ready, it)
                at_least(pe, log_probs, q + 1)
                if softmax_bank(q) == 7:
                    at_least(pe, pooledT_ready, q)
                else:
                    pe.wait_ge(hT_ready, 4 * NQ)
                into = bank[softmax_bank(q)]
                for t in range(NK):
                    ins = pe.transpose(into[0:TR, t * P:(t + 1) * P], log_p[:, t * TR:(t + 1) * TR], ident[:, :])
                ins.then_inc(log_pT, 1)

            def turn_scores(q):
                at_least(pe, din_probs, q + 1)
                at_least(pe, log_w, q + 1)
                for t in range(SIDE // TR):
                    ins = pe.transpose(bank[softmax_bank(q)][0:TR, t * P:(t + 1) * P], din_p[:, t * TR:(t + 1) * TR], ident[:, :])
                ins.then_inc(din_pT, 1)

            def pool_rows(q, k):
                at_least(pe, din_w, q + 1)
                for r in range(2):
                    for odd in range(2):
                        for c in range(NK):
                            t = r * (QT // 2) + 2 * c + odd
                            ins = mm(bank[softmax_bank(q)][32 * c:32 * c + 32, r * D:(r + 1) * D],
                                     p_w[0:TR, t, (16, 0)[odd]:(16, 0)[odd] + 32],
                                     hist[0:TR, k, t, :], odd == 0, odd == 1)
                ins.then_inc(pool_done, 1)

            def turn_pooled(q):
                at_least(pe, pooled_ready, q + 1)
                for c in range(C):
                    for r in range(2):
                        ins = pe.transpose(bank[softmax_bank(q)][:, (2 * c + r) * P:(2 * c + r + 1) * P],
                                           pooled[:, r, c * P:(c + 1) * P], ident[:, :])
                ins.then_inc(pooledT, 1)

            def block_values(into, n0=0, n1=P):
                for et in range(C):
                    for c in range(C):
                        for h in (2 * et, 2 * et + 1):
                            ins = mm(into[(h % 2) * HD:(h % 2 + 1) * HD, et * P + n0:et * P + n1],
                                     wvT[:, c, h * HD:(h + 1) * HD],
                                     view(headT, c * P * H + n0 * H + h, [(H, n1 - n0)]), c == 0, c == C - 1)
                ins.then_inc(v_done, 1)

            def mix_interest(into, interest, first):
                for c in range(C):
                    mm(into[:, 0:D], interest[:, c, :], woT[:, c, :], first and c == 0, False)

            def mix_values(into):
                for c in range(C):
                    ins = mm(into[:, 0:D], vT[:, c, :], w_mix[:, c, :], False, c == C - 1)
                ins.then_inc(z_done, 1)

            def step(q, k, it=0):
                one, two = (k - 1) % RING, (k - 2) % RING
                here = lambda back: not isinstance(q, int) or 0 <= q - back < NQ
                if here(0):
                    turn(q, k, 0, it)
                if isinstance(q, int) and q == 0:
                    query_part()
                if isinstance(q, int) and q == 1:
                    pe.wait_ge(kq_kept, H * C)
                    pe.wait_ge(mix_kept, 1)
                    pe.wait_ge(b_mix_ready, 1)
                if here(1):
                    first_layer(q - 1, one, 1)
                if here(2):
                    turn_scores(q - 2)
                if here(1):
                    second_layer(q - 1, one, 0)
                    quad_logits(q - 1, one)
                    second_layer(q - 1, one, 1)
                if here(2):
                    pool_rows(q - 2, two)
                if here(0):
                    turn(q, k, 1, it, (0,))
                if here(1):
                    quad_scores(q - 1, one)
                if here(2):
                    turn_pooled(q - 2)
                if here(0):
                    turn(q, k, 1, it, (1,))
                if not isinstance(it, int) and k == 1:
                    at_least(pe, pooledT_ready, RING * it)
                    block_values(bank[7])
                if not isinstance(it, int) and k == 2:
                    at_least(pe, pooledT_ready, q - 1)
                    at_least(pe, interest_kept, it)
                    mix_interest(bank[7], interest_k, True)
                    at_least(pe, v_ready, it)
                    mix_values(bank[7])
                if here(0):
                    first_layer(q, k, 0)
                if here(1):
                    turn_logits(q - 1, one, it)

            start_layer1()
            step(0, 0)
            prepare_heads()
            for k in range(1, RING):
                step(k, k)
            with pe.Fori(1, NQ // RING) as it:
                for k in range(RING):
                    step(it * RING + k, k, it)
            step(NQ, 0)
            pe.wait_ge(pooledT_ready, NQ - 1)
            block_values(bank[2], 0, P - QB)
            mm(bank[0][:, 0:D], ident[:, :], b_mix[:, :], True, False)
            step(NQ + 1, 1)
            pe.wait_ge(pooledT_ready, NQ)
            pe.wait_ge(v_ready, BB)
            block_values(bank[2], P - QB, P)
            mix_interest(bank[0], interestT, False)
            pe.wait_ge(v_ready, BB + 1)
            mix_values(bank[0])

        @block.scalar
        def _(act):
            for dst, src in ((a1_c, a1), (a2_c, a2)):
                act.dma_start(dst[:, :], src.unsqueeze(0).to_broadcast([P, 1])).then_inc(ld_prelu, 16)
            for dst, src in ((b1_c, b1), (b2_c, b2)):
                act.dma_start(dst[:, :], src.unsqueeze(1).unsqueeze(0).to_broadcast([2, A, 1])).then_inc(ld_bias, 16)

            def keep_weight(dst, src):
                return act.copy(dst.rearrange("p c e -> p (c e)"), src[:, :])

            def keep_query():
                for c in range(C):
                    act.wait_ge(query_turned, 1 + c)
                    act.copy(qT[:, c, :], bank[c][:, :]).then_inc(query_kept, 1)

            def keep_heads():
                act.wait_ge(ld_small, 16 * 3)
                for t in range(C):
                    act.wait_ge(q_done, 1 + t)
                    act.activation(q_e[:, t, :], bank[6 + t][:, :], ACT.Identity,
                                   bias=inb_c[:, t:t + 1]).then_inc(q_kept, 1)
                act.wait_ge(wv_turned, 1)
                keep_weight(wvT[:, :, :], bank[5]).then_inc(wv_kept, 1)
                act.wait_ge(wo_turned, 1)
                keep_weight(woT[:, C:2 * C, :], bank[4]).then_inc(wo_kept, 1)
                for i in range(H * C):
                    if i == 4:
                        act.wait_ge(wo_turned, 2)
                        keep_weight(woT[:, 0:C, :], bank[6]).then_inc(wo_kept, 1)
                    act.wait_ge(kq_done, 1 + i)
                    h, c = i // C, i % C
                    act.copy(view(kq, c * B * H + h, [(H, B)]), bank[(7, 5)[i % 2]][:, :]).then_inc(kq_kept, 1)
                act.wait_ge(mix_done, 1)
                keep_weight(w_mix[:, :, :], bank[4]).then_inc(mix_kept, 1)

            def take_turned(q, k, r):
                for ab in range(2):
                    at_least(act, turned, 4 * q + 2 * r + ab + 1)
                    act.copy(view(hT, (((k % 2) * 2 + r) * C) * 2 * GR + ab * GR, [(2 * GR, C), (1, GR)]),
                             psum[:, 2 * ab:2 * ab + 2, 0:GR]).then_inc(hT_ready, 1)

            def add_b2(q, r):
                at_least(act, layer2, 2 * q + r + 1)
                act.activation(h2[:, r, :], bank[4 + r][:, 0:GR], ACT.Identity, bias=b2_s[:, :]).then_inc(h2_sum, 1)

            def exp_logits(q):
                at_least(act, log_masked, q + 1)
                act.activation(log_p[:, :], log_t[:, :], ACT.Exp, bias=small[:, 0:1], scale=-1.0,
                               accum_out=small[:, 1:2]).then_inc(log_exp, 1)

            def exp_scores(q):
                at_least(act, din_masked, q + 1)
                act.activation(din_p[:, :], din_t[:, :], ACT.Exp, bias=small[:, 2:3], scale=-1.0,
                               accum_out=small[:, 3:4]).then_inc(din_exp, 1)

            def take_pooled(q):
                at_least(act, pool_done, q + 1)
                act.copy(pooled[:, :, :].rearrange("p r d -> p (r d)"), bank[softmax_bank(q)][:, :]).then_inc(pooled_ready, 1)

            def take_values(count, src=bank[7], n0=0, n1=P):
                at_least(act, v_done, count)
                for et in range(C):
                    ins = act.activation(vT[:, et, n0:n1], src[:, et * P + n0:et * P + n1], ACT.Identity,
                                         bias=inb_c[:, 2 * C + et:2 * C + et + 1])
                ins.then_inc(v_ready, 1)

            def step(q, k, it=0):
                here = lambda back: not isinstance(q, int) or 0 <= q - back < NQ
                if here(0):
                    take_turned(q, k, 0)
                if isinstance(q, int) and q == 0:
                    act.wait_ge(wq_turned, 1)
                    keep_weight(wqT[:, :, :], bank[6]).then_inc(wq_kept, 1)
                if here(1):
                    add_b2(q - 1, 0)
                    add_b2(q - 1, 1)
                    exp_logits(q - 1)
                if here(2):
                    take_pooled(q - 2)
                if here(0):
                    take_turned(q, k, 1)
                if here(1):
                    exp_scores(q - 1)
                if not isinstance(it, int) and k == 1:
                    take_values(it)

            keep_query()
            step(0, 0)
            keep_heads()
            for k in range(1, RING):
                step(k, k)
            with act.Fori(1, NQ // RING) as it:
                for k in range(RING):
                    step(it * RING + k, k, it)
            step(NQ, 0)
            take_values(BB, bank[2], 0, P - QB)
            step(NQ + 1, 1)
            take_values(BB + 1, bank[2], P - QB, P)

        @block.vector
        def _(dve):
            for zeros in (w2T[:, :], q_x[:, :, :, :], bk_x[:, :, :], w3_x[:, :], p_w[:, :, :]):
                dve.memset(zeros, 0.0).then_inc(cleared_v, 1)
            dve.wait_ge(ld_w1, 16)
            dve.tensor_tensor(w1_c[:, 0, :], w1_n[:, 0, :], w1_n[:, 2, :], ALU.add)
            dve.tensor_tensor(w1_c[:, 1, :], w1_n[:, 1, :], w1_n[:, 2, :], ALU.subtract).then_inc(prepared, 1)
            dve.wait_ge(ld_prelu, 16 * 2)
            for i, a in enumerate((a1_c, a2_c)):
                dve.tensor_scalar(sign[:, i:i + 1], a[:, :], 1.0, 2.0, ALU.is_le, ALU.mult).then_inc(signs, 1)
            dve.wait_ge(signs, 2)
            dve.tensor_scalar(sign[:, 3:5], sign[:, 0:2], -1.0, None, ALU.add).then_inc(signs, 1)
            dve.wait_ge(signs, 3)
            sign1, sign2 = sign[:, 3:4], sign[:, 4:5]
            dve.tensor_tensor(sign[:, 5:6], sign1, sign2, ALU.mult).then_inc(signs, 1)
            dve.wait_ge(w1_turned, 1)
            dve.tensor_scalar(w1T[:, :, :].rearrange("p i a -> p (i a)"), bank[5][:, 0:4 * A], sign1, None,
                              ALU.mult).then_inc(w1T_ready, 1)
            dve.tensor_scalar(w1uT[:, :, :].rearrange("p c a -> p (c a)"), bank[5][:, 4 * A:6 * A], sign1, None,
                              ALU.mult).then_inc(w1T_ready, 1)

            def keep_query_part():
                dve.wait_ge(ld_bias, 16 * 2)
                dve.tensor_tensor(b1_s[:, :], b1_c[:, :], sign1, ALU.mult).then_inc(signs, 1)
                dve.tensor_tensor(b2_s[:, :], b2_c[:, :], sign2, ALU.mult).then_inc(signs, 1)
                dve.wait_ge(signs, 6)
                dve.wait_ge(u_done, 1)
                dve.tensor_scalar(u[:, :, :].rearrange("p n e -> p (n e)"), bank[7][:, 0:B // 2], b1_s[:, :], None,
                                  ALU.add).then_inc(u_ready, 1)
                dve.wait_ge(w2_turned, 1)
                dve.wait_ge(cleared_v, 5)
                for r in range(2):
                    ins = dve.tensor_scalar(w2T[r * A:(r + 1) * A, r * A:(r + 1) * A], bank[5][r * A:(r + 1) * A, 0:A],
                                            sign[r * A:(r + 1) * A, 5:6], None, ALU.mult)
                ins.then_inc(w2T_ready, 1)
                dve.wait_ge(ld_mask, 16)
                dve.tensor_scalar(mask_b[:, :, :], mask_i[:, :, :], 0.0, -1.0, ALU.not_equal,
                                  ALU.add).then_inc(mask_ready, 1)
                dve.wait_ge(ld_small, 16 * 3)
                for r in range(2):
                    dve.tensor_scalar(w3_x[r * A:(r + 1) * A, 16 * r:16 * r + GB // 2],
                                      w3_c[r * A:(r + 1) * A, :].to_broadcast([A, GB // 2]),
                                      sign[r * A:(r + 1) * A, 4:5], None, ALU.mult)
                for h in range(H):
                    r = h % 2
                    ins = dve.tensor_copy(bk_x[r * HD:(r + 1) * HD, h // 2, h:h + 1],
                                          inb_c[r * HD:(r + 1) * HD, C + h // 2:C + h // 2 + 1])
                ins.then_inc(bk_ready, 1)
                dve.wait_ge(u_ready, 1)

            def keep_heads():
                for t in range(C):
                    dve.wait_ge(q_kept, 1 + t)
                    for r in range(2):
                        ins = dve.tensor_scalar(q_x[r * HD:(r + 1) * HD, r, t, :],
                                                bank[6 + t][r * HD:(r + 1) * HD, :],
                                                inb_c[r * HD:(r + 1) * HD, t:t + 1], None, ALU.add)
                    ins.then_inc(q_ready, 1)
                dve.wait_ge(qbk_done, 1)
                dve.tensor_copy(qbk_r[:, :, :], bank[6][0:H, :].rearrange("h (q b) -> h b q", b=QB)
                                ).then_inc(qbk_rows, 1)
                dve.wait_ge(ld_rows, 16 * 5)
                dve.tensor_copy(outb_x[:, :, :], outb_c[:, :].unsqueeze(2).to_broadcast([P, C, P])
                                ).then_inc(outb_ready, 1)
                half = NQ // 2
                dve.wait_ge(own_done, 4)
                for i in range(2):
                    dve.tensor_scalar(own_din[:, i * half:(i + 1) * half, :],
                                      bank[2 + i][:, 0:half * S].rearrange("p (q s) -> p q s", s=S), BIG,
                                      b3_c[:, :], ALU.mult, ALU.add).then_inc(own_ready, 1)
                for m, src in ((other_log[:, :], bank[0][:, half * S:half * S + GB]),
                               (other_din[:, :], bank[2][:, half * S:half * S + GB // 2])):
                    dve.tensor_scalar(m, src, -1.0, BIG, ALU.add, ALU.mult).then_inc(own_ready, 1)
                dve.wait_ge(qbk_moved, 16 * H)
                for i in range(2):
                    dve.scalar_tensor_tensor(
                        own_log[:, i * half:(i + 1) * half, :],
                        bank[i][:, 0:half * S].rearrange("p (q s) -> p q s", s=S), BIG,
                        qbk[:, i * half:(i + 1) * half].unsqueeze(2).to_broadcast([P, half, S]),
                        ALU.mult, ALU.add).then_inc(own_ready, 1)
                dve.wait_ge(b_mix_done, 1)
                dve.tensor_tensor(b_mix[:, :], bank[6][:, 0:D], bo_b[:, :], ALU.add).then_inc(b_mix_ready, 1)

            def times_query(q, k, r):
                for ab in range(2):
                    g = 4 * q + 2 * r + ab
                    at_least(dve, hT_ready, g + 1)
                    off, dims = r * C * 2 * GR + ab * GR, [(2 * GR, C), (S, GB), (1, S)]
                    dve.tensor_tensor(view(qhT, off, dims), view(hT, (k % 2) * 2 * C * 2 * GR + off, dims),
                                      qT[:, :, bass.ds(g * GB, GB)].unsqueeze(3).to_broadcast([P, C, GB, S]),
                                      ALU.mult).then_inc(qhT_ready, 1)

            def add_query(q, r):
                at_least(dve, layer1, 2 * q + r + 1)
                dve.tensor_tensor(h1[:, r, :].rearrange("p (e s) -> p e s", s=S),
                                  bank[4 + r][:, 0:GR].rearrange("p (e s) -> p e s", s=S),
                                  u[:, bass.ds(2 * q + r, 1), :].rearrange("p n e -> p (n e)").unsqueeze(2)
                                  .to_broadcast([P, GB, S]), ALU.add).then_inc(h1_sum, 1)

            def prelu1(q, r):
                at_least(dve, h1_sum, 2 * q + r + 1)
                dve.scalar_tensor_tensor(h1[:, r, :], h1[:, r, :], a1_c[:, :], h1[:, r, :], ALU.mult,
                                         ALU.max).then_inc(h1_ready, 1)

            def prelu2(q, r):
                at_least(dve, h2_sum, 2 * q + r + 1)
                dve.scalar_tensor_tensor(h2[:, r, :], h2[:, r, :], a2_c[:, :], h2[:, r, :], ALU.mult,
                                         ALU.max).then_inc(h2_ready, 1)

            def mask_logits(q, k):
                dve.wait_ge(qbk_moved, 16 * H)
                at_least(dve, logits, q + 1)
                at_least(dve, quad_masks, 2 * q + 2)
                dve.tensor_tensor_reduce(log_t[:, :], bank[6][:, 0:GR], mask_log[:, k % 2, :],
                                         -1.0 / HD ** 0.5, 3e38, ALU.add, ALU.min,
                                         small[:, 0:1]).then_inc(log_masked, 1)

            def mask_scores(q, k):
                dve.wait_ge(qbk_moved, 16 * H)
                at_least(dve, scores, q + 1)
                at_least(dve, quad_masks, 2 * q + 2)
                dve.tensor_tensor_reduce(din_t[:, :], bank[4][:, 0:SIDE], mask_din[:, k % 2, :], -1.0, 3e38,
                                         ALU.add, ALU.min, small[:, 2:3]).then_inc(din_masked, 1)

            def normalise_logits(q):
                at_least(dve, log_exp, q + 1)
                dve.reciprocal(small[:, 4:5], small[:, 1:2]).then_inc(recips, 1)
                at_least(dve, recips, 2 * q + 1)
                dve.tensor_scalar(log_p[:, :], log_p[:, :], small[:, 4:5], None, ALU.mult).then_inc(log_probs, 1)

            def normalise_scores(q):
                at_least(dve, din_exp, q + 1)
                dve.reciprocal(small[:, 5:6], small[:, 3:4]).then_inc(recips, 1)
                at_least(dve, recips, 2 * q + 2)
                dve.tensor_scalar(din_p[:, :], din_p[:, :], small[:, 5:6], None, ALU.mult).then_inc(din_probs, 1)

            def place_logits(q):
                at_least(dve, log_pT, q + 1)
                dve.tensor_copy(view(p_w, 16, [(NK * PW, 4), (PW, NK), (1, 8)], TR),
                                view(psum, softmax_bank(q) * 512, [(32, 4), (P + 8, NK), (1, 8)], TR)).then_inc(log_w, 1)

            def place_scores(q):
                at_least(dve, din_pT, q + 1)
                dve.tensor_copy(view(p_w, 24, [(2 * PW, QT // 2), (PW, 2), (1, 2)], TR),
                                view(psum, softmax_bank(q) * 512, [(16, QT // 2), (P + 2, 2), (1, 2)], TR)).then_inc(din_w, 1)

            def take_pooledT(q, k, it):
                if k == 0:
                    at_least(dve, v_done, it)
                    at_least(dve, interest_kept, it)
                at_least(dve, pooledT, q + 1)
                src = bank[softmax_bank(q)][:, :].rearrange("p (c t x) -> p c t x", c=C, x=16)
                dve.tensor_copy(headT[:, :, k * P:(k + 1) * P].rearrange("p c (t x) -> p c t x", x=8),
                                src[:, :, :, 0:8])
                dve.tensor_copy(interestT[:, :, k * QB:(k + 1) * QB].rearrange("p c (t x) -> p c t x", x=2),
                                src[:, :, :, 8:10]).then_inc(pooledT_ready, 1)

            def block_moments(count):
                at_least(dve, z_done, count)
                dve.tensor_tensor(z[:, :], bank[7][:, 0:D], b_mix[:, :], ALU.add).then_inc(z_ready, 1)
                at_least(dve, z_ready, count)
                dve.bn_stats(stats[:, :], z[:, :]).then_inc(z_stats, 1)
                dve.wait_ge(qbk_moved, 16 * H)
                at_least(dve, z_stats, count)
                dve.bn_aggr(moments[:, :], stats[:, :]).then_inc(z_moments, 1)
                at_least(dve, z_moments, 2 * count - 1)
                dve.tensor_scalar(rstd[:, 0:1], moments[:, 1:2], EPS, None, ALU.add).then_inc(z_moments, 1)

            def step(q, k, it=0):
                one = (k - 1) % RING
                here = lambda back: not isinstance(q, int) or 0 <= q - back < NQ
                if isinstance(q, int) and q == 0:
                    dve.wait_ge(query_kept, C)
                if here(0):
                    times_query(q, k, 0)
                if isinstance(q, int) and q == 0:
                    keep_query_part()
                if here(1):
                    add_query(q - 1, 1)
                if here(2):
                    place_scores(q - 2)
                if here(1):
                    prelu1(q - 1, 1)
                    prelu2(q - 1, 0)
                    mask_logits(q - 1, one)
                    prelu2(q - 1, 1)
                    normalise_logits(q - 1)
                    mask_scores(q - 1, one)
                if here(2):
                    take_pooledT(q - 2, (k - 2) % RING, it)
                if here(0):
                    times_query(q, k, 1)
                if here(1):
                    normalise_scores(q - 1)
                if not isinstance(it, int) and k == 2:
                    block_moments(it)
                if here(0):
                    add_query(q, 0)
                if here(1):
                    place_logits(q - 1)
                if here(0):
                    prelu1(q, 0)

            step(0, 0)
            keep_heads()
            for k in range(1, RING):
                step(k, k)
            with dve.Fori(1, NQ // RING) as it:
                for k in range(RING):
                    step(it * RING + k, k, it)
            step(NQ, 0, 0)
            step(NQ + 1, 1, 0)
            z_last = bank[0][:, 0:D]
            dve.wait_ge(z_done, BB)
            dve.bn_stats(stats[:, :], z_last).then_inc(z_stats, 1)
            dve.wait_ge(y_ready, BB - 1)
            dve.wait_ge(stored, 16 * (BB - 1))
            dve.wait_ge(z_stats, BB)
            dve.bn_aggr(moments[:, :], stats[:, :]).then_inc(z_moments, 1)
            dve.wait_ge(z_moments, 2 * BB - 1)
            dve.tensor_scalar(rstd[:, 0:1], moments[:, 1:2], EPS, None, ALU.add).then_inc(z_moments, 1)
            dve.scalar_tensor_tensor(zn[:, :], z_last, moments[:, 0:1], lnw_b[:, :], ALU.subtract,
                                     ALU.mult).then_inc(z_norm, 1)
            dve.wait_ge(z_norm, BB)
            dve.wait_ge(z_rstd, BB)
            dve.scalar_tensor_tensor(zn[:, :], zn[:, :], rstd[:, 1:2], lnb_b[:, :], ALU.mult,
                                     ALU.add).then_inc(z_shifted, 1)
            dve.wait_ge(z_shifted, BB)
            dve.tensor_scalar(y[:, :], zn[:, :], 0.0, ao_c[:, :], ALU.min, ALU.mult).then_inc(z_below, 1)
            dve.wait_ge(z_below, BB)
            dve.scalar_tensor_tensor(y[:, :], zn[:, :], 0.0, y[:, :], ALU.max, ALU.add).then_inc(y_ready, 1)


_INS = ['r_history_mask', 'L0_rec_query', 'L0_rec_history', 'L0_rec_W1', 'L0_rec_b1', 'L0_rec_a1', 'L0_rec_W2',
        'L0_rec_b2', 'L0_rec_a2', 'L0_rec_W3', 'L0_rec_b3', 'L0_rec_in_w', 'L0_rec_in_b', 'L0_rec_out_w',
        'L0_rec_out_b', 'L0_rec_Wo', 'L0_rec_bo', 'L0_rec_ln_w', 'L0_rec_ln_b', 'L0_rec_ao']


def kernel(**inputs):
    import numpy as _np
    import concourse.bacc as _bacc
    from concourse import mybir as _mybir
    from concourse.bass_utils import run_bass_kernel_spmd as _run

    nc = _bacc.Bacc("TRN2", target_bir_lowering=False, num_devices=1)
    arrays, args = {}, []
    for name in _INS:
        a = _np.ascontiguousarray(inputs[name])
        a = a.reshape(a.shape or (1,))
        arrays[f"in_{name}_dram"] = a
        args.append(nc.dram_tensor(f"in_{name}_dram", a.shape, _mybir.dt.from_np(a.dtype), kind="ExternalInput").ap())
    shape = inputs['L0_rec_query'].shape
    args.append(nc.dram_tensor("out_0_dram", shape, F32, kind="ExternalOutput").ap())
    rec_kernel(nc, *args)
    r = _run(nc, [arrays], core_ids=[0])
    return r.results[0]["out_0_dram"]
```

```python
from contextlib import ExitStack

import concourse.bass as bass
from concourse import mybir

F32 = mybir.dt.float32
BF16 = mybir.dt.bfloat16
I32 = mybir.dt.int32
ALU = mybir.AluOpType
ACT = mybir.ActivationFunctionType

COLUMNS = dict(w2=(0, 64), b1=(64, 65), b2=(65, 66), w3=(66, 67), a1=(67, 68), a2=(68, 69), ao=(69, 70),
               b3=(70, 71), in_b=(71, 77), out_b=(77, 79))

BIG = 1e30
EPS = 1e-5


def at_least(engine, semaphore, count):
    if isinstance(count, int) and count <= 0:
        return
    engine.wait_ge(semaphore, count)


def rec_kernel(nc, mask, query, history, w1_t, wq_t, wk, wv_t, out_w, wo_t, columns, rows, out):
    B, S, D = history.shape
    A = w1_t.shape[1]
    H = 4
    HD = D // H
    P = 128
    C = D // P
    GB = 8
    GR = GB * S
    TR = 2 * S
    NK = GR // TR
    QB = 4 * GB
    QT = 4 * NK
    NQ = B // QB
    RING = 4
    BB = B // P
    SIDE = GB // 2 * S
    PW = 48
    WARM_UP = 14
    STAY_WARM = 7
    assert (C, A, HD, TR, NQ % RING, RING * QB) == (2, 64, 64, 100, 0, P)

    hist_v = history.rearrange("(q r t e) s d -> q r (e s) t d", r=2, t=QT // 2, e=2)

    with ExitStack() as ctx:
        def sb(name, shape, dt=F32):
            return ctx.enter_context(nc.sbuf_tensor(name, shape, dt))

        def sem(name):
            return ctx.enter_context(nc.semaphore(name))

        hist = sb("hist", [P, RING, QT, D])
        hT = sb("hT", [P, 2, 2, C, 2 * GR])
        qhT = sb("qhT", [P, 2, C, 2 * GR])
        h1 = sb("h1", [P, 2, GR])
        h2 = sb("h2", [P, 2, GR])
        log_t = sb("log_t", [P, GR])
        log_p = sb("log_p", [P, GR])
        din_t = sb("din_t", [P, SIDE])
        din_p = sb("din_p", [P, SIDE])
        small = sb("small", [P, 8])
        p_w = sb("p_w", [P, QT, PW])
        pooled = sb("pooled", [P, 2, D])
        headT = sb("headT", [P, C, P * H])
        interestT = sb("interestT", [P, C, P])
        kq = sb("kq", [P, C, B * H])
        kq_quad = sb("kq_quad", [P, 2, C, P])
        mask_log = sb("mask_log", [P, 2, GR])
        mask_din = sb("mask_din", [P, 2, SIDE])
        own_log = sb("own_log", [P, NQ, S])
        own_din = sb("own_din", [P, NQ, S])
        other_log = sb("other_log", [P, GB])
        other_din = sb("other_din", [P, GB // 2])
        ident = sb("ident", [P, P])
        mask_i = sb("mask_i", [QB, NQ, S], I32)
        mask_b = sb("mask_b", [QB, NQ, S], BF16)
        to_log = sb("to_log", [QB, GB // 2, GB, H], BF16)
        to_din = sb("to_din", [QB, GB, 16], BF16)
        of_group = sb("of_group", [QB, GB], BF16)
        of_side = sb("of_side", [QB, GB // 2], BF16)
        query_n = hist[:, RING - 1, 0:BB, :]
        wk_n = hist[:, RING - 1, 4:4 + C, :]
        outw_n = hist[:, RING - 1, 8:8 + C, :]
        qT = sb("qT", [P, C, B])
        w1_n = sb("w1_n", [P, 4, C, A])
        w1_c = sb("w1_c", [P, 2, C, A])
        w1T = sb("w1T", [P, 2 * C, A])
        w1uT = sb("w1uT", [P, C, A])
        u = sb("u", [P, 2 * NQ, GB])
        columns_c = sb("columns_c", [P, columns.shape[1]])
        w2_c, b1_c, b2_c, w3_c, a1_c, a2_c, ao_c, b3_c, inb_c, outb_c = (
            columns_c[:, COLUMNS[n][0]:COLUMNS[n][1]]
            for n in ("w2", "b1", "b2", "w3", "a1", "a2", "ao", "b3", "in_b", "out_b"))
        sign = sb("sign", [P, 8])
        b1_s = sb("b1_s", [P, 1])
        b2_s = sb("b2_s", [P, 1])
        w2T = sb("w2T", [P, P])
        w3_x = sb("w3_x", [P, 32])
        bk_x = sb("bk_x", [P, C, 32])
        wqT = sb("wqT", [P, C, D])
        wvT = sb("wvT", [P, C, D])
        early = hT[:, 1, :, :, :].rearrange("p r c n -> p (r c n)")
        q_x = early[:, 0:2 * C * B].rearrange("p (r c b) -> p r c b", r=2, c=C)
        q_e = early[:, 2 * C * B:3 * C * B].rearrange("p (c b) -> p c b", c=C)
        qbk_r = sb("qbk_r", [P, QB, RING])
        qbk = sb("qbk", [P, NQ])
        outb_x = sb("outb_x", [P, C, P])
        woT = sb("woT", [P, 2 * C, D])
        w_mix = sb("w_mix", [P, C, D])
        b_mix = sb("b_mix", [P, D])
        rows_b = sb("rows_b", [P, 3, D])
        bo_b, lnw_b, lnb_b = (rows_b[:, i, :] for i in range(3))
        vT = sb("vT", [P, C, P])
        interest_k = sb("interest_k", [P, C, P])
        z = sb("z", [P, D])
        zn = sb("zn", [P, D])
        y = sb("y", [P, D])
        stats = sb("stats", [P, 6])
        moments = sb("moments", [P, 2])
        rstd = sb("rstd", [P, 2])
        minus_half = sb("minus_half", [P, 1])

        psum = ctx.enter_context(nc.psum_tensor("psum", [P, 8, 512], F32))
        bank = [psum[:, i, :] for i in range(8)]

        def view(t, offset, dims, parts=P, start=0):
            base = t[start:start + parts]
            free = 1
            for n in t.shape[1:]:
                free *= n
            return bass.AP(base.tensor, base.offset + offset, [[free, parts]] + [list(d) for d in dims])

        ld_query, ld_columns, ld_w1, ld_wq, ld_wk, ld_late, ld_mask, ld_rows = (
            sem("ld_query"), sem("ld_columns"), sem("ld_w1"), sem("ld_wq"), sem("ld_wk"), sem("ld_late"),
            sem("ld_mask"), sem("ld_rows"))
        ld_hist = [[sem(f"ld_hist{k}{r}") for r in range(2)] for k in range(RING)]
        consts, cleared = sem("consts"), sem("cleared")
        cleared_v, prepared = sem("cleared_v"), sem("prepared")
        query_turned, q_done, u_done, own_done = sem("query_turned"), sem("q_done"), sem("u_done"), sem("own_done")
        qbk_done, kq_done, mix_done, b_mix_done = sem("qbk_done"), sem("kq_done"), sem("mix_done"), sem("b_mix_done")
        query_kept, q_kept, kq_kept, mix_kept = sem("query_kept"), sem("q_kept"), sem("kq_kept"), sem("mix_kept")
        w1T_ready, u_ready, w2T_ready, bk_ready, mask_ready, q_ready, qbk_rows, own_ready, outb_ready, b_mix_ready = (
            sem("w1T_ready"), sem("u_ready"), sem("w2T_ready"), sem("bk_ready"), sem("mask_ready"), sem("q_ready"),
            sem("qbk_rows"), sem("own_ready"), sem("outb_ready"), sem("b_mix_ready"))
        qbk_moved = sem("qbk_moved")
        turned = sem("turned")
        hT_ready = sem("hT_ready")
        qhT_ready = sem("qhT_ready")
        layer1 = sem("layer1")
        h1_sum = sem("h1_sum")
        h1_ready = sem("h1_ready")
        layer2 = sem("layer2")
        h2_sum = sem("h2_sum")
        h2_ready = sem("h2_ready")
        signs = sem("signs")
        logits = sem("logits")
        scores = sem("scores")
        log_masked, din_masked = sem("log_masked"), sem("din_masked")
        log_exp, din_exp = sem("log_exp"), sem("din_exp")
        log_probs, din_probs = sem("log_probs"), sem("din_probs")
        recips = sem("recips")
        log_pT, din_pT = sem("log_pT"), sem("din_pT")
        log_w, din_w = sem("log_w"), sem("din_w")
        pool_done = sem("pool_done")
        pooled_ready = sem("pooled_ready")
        pooledT = sem("pooledT")
        pooledT_ready = sem("pooledT_ready")
        quad_kq = sem("quad_kq")
        quad_masks = sem("quad_masks")
        v_done, v_ready, interest_kept = sem("v_done"), sem("v_ready"), sem("interest_kept")
        z_done, z_ready, z_stats, z_moments = sem("z_done"), sem("z_ready"), sem("z_stats"), sem("z_moments")
        z_eps, z_rstd, z_norm, z_scaled, z_shifted = (
            sem("z_eps"), sem("z_rstd"), sem("z_norm"), sem("z_scaled"), sem("z_shifted"))
        z_below, z_above, y_ready = sem("z_below"), sem("z_above"), sem("y_ready")
        stored, last_stored = sem("stored"), sem("last_stored")

        block = ctx.enter_context(nc.Block())

        def softmax_bank(q):
            return 1 if isinstance(q, int) and q == NQ - 1 else 7

        @block.sync
        def _(sp):
            def load(q, k, r):
                at_least(sp, pool_done, q - RING + 1)
                sp.dma_start(hist[0:TR, k, r * (QT // 2):(r + 1) * (QT // 2), :],
                             hist_v[q, r]).then_inc(ld_hist[k][r], 16)

            def load_weight(dst, src, signal):
                sp.dma_start(dst, src.rearrange("(t p) d -> p t d", p=P)).then_inc(signal, 16)

            load_weight(query_n, query, ld_query)
            load_weight(wqT[:, :, :], wq_t, ld_wq)
            load(0, 0, 0)
            load(0, 0, 1)
            load_weight(wk_n, wk, ld_wk)
            load_weight(outw_n, out_w, ld_late)
            load_weight(woT[:, :, :], wo_t, ld_late)
            for r in range(2):
                load(1, 1, r)
            load_weight(wvT[:, :, :], wv_t, ld_late)
            sp.wait_ge(qbk_rows, 1)
            for j in range(BB):
                for h in range(H):
                    to = qbk[h:h + 1, j * RING:(j + 1) * RING]
                    sp.dma_start(bass.AP(to.tensor, to.offset, [[H * NQ, QB], [1, RING]]),
                                 qbk_r[32 * j + h:32 * j + h + 1, :, :]).then_inc(qbk_moved, 16)
            for r in range(2):
                load(2, 2, r)
            sp.wait_ge(mix_done, 1)
            for r in range(2):
                load(RING - 1, RING - 1, r)
            with sp.Fori(1, NQ // RING) as it:
                for k in range(RING):
                    for r in range(2):
                        load(it * RING + k, k, r)
            sp.wait_ge(y_ready, BB)
            sp.dma_start(out[(BB - 1) * P:BB * P, :], y[:, :]).then_inc(last_stored, 16)
            sp.wait_ge(stored, 16 * (BB - 1))
            sp.wait_ge(last_stored, 16)

        @block.gpsimd
        def _(pool):
            pool.memset(ident[:, :], 0.0).then_inc(cleared, 1)
            pool.wait_ge(cleared, 1)
            pool.affine_select(out=ident[:, :], in_=ident[:, :], compare_op=ALU.not_equal, fill=1.0, base=0,
                               pattern=[[-1, P]], channel_multiplier=1).then_inc(consts, 1)

            pool.dma_start(mask_i[:, :, :], mask.rearrange("(q b) s -> b q s", b=QB)).then_inc(ld_mask, 16)
            pool.memset(to_log[:, :, :, :], 0.0).then_inc(cleared, 1)
            pool.memset(to_din[:, :, :], 0.0).then_inc(cleared, 1)
            pool.memset(of_group[:, :], 0.0).then_inc(cleared, 1)
            pool.memset(of_side[:, :], 0.0).then_inc(cleared, 1)
            pool.wait_ge(cleared, 5)
            pool.affine_select(out=to_log[:, :, :, :], in_=to_log[:, :, :, :], compare_op=ALU.not_equal, fill=1.0,
                               base=0, pattern=[[-GB, 4], [-1, GB], [0, H]], channel_multiplier=1).then_inc(consts, 1)
            pool.affine_select(out=to_din[:, :, 0:GB // 2], in_=to_din[:, :, 0:GB // 2], compare_op=ALU.not_equal,
                               fill=1.0, base=0, pattern=[[-GB // 2, GB], [-1, GB // 2]],
                               channel_multiplier=1).then_inc(consts, 1)
            for step_, sel in ((GB, of_group), (GB // 2, of_side)):
                for g in range(QB // step_):
                    pool.affine_select(out=sel[:, :], in_=sel[:, :], compare_op=ALU.not_equal, fill=1.0,
                                       base=-step_ * g, pattern=[[-1, step_]],
                                       channel_multiplier=1).then_inc(consts, 1)
                    pool.wait_ge(consts, 4 + g + (0 if sel is of_group else 4))
            pool.dma_start(rows_b[:, :, :].rearrange("p i d -> p (i d)"),
                           rows.rearrange("i d -> (i d)").unsqueeze(0).to_broadcast([P, 3 * D])).then_inc(ld_rows, 16)
            pool.memset(minus_half[:, :], -0.5).then_inc(z_eps, 1)

            def quad(q, k):
                at_least(pool, logits, q - 1)
                pool.tensor_copy(kq_quad[:, k % 2, :, :],
                                 kq[:, :, bass.ds(q * P, P)]).then_inc(quad_kq, 1)
                at_least(pool, log_masked, q - 1)
                at_least(pool, din_masked, q - 1)
                for m, own, other, n in ((mask_log, own_log, other_log, GB), (mask_din, own_din, other_din, GB // 2)):
                    pool.tensor_tensor(m[:, k % 2, :].rearrange("p (e s) -> p e s", s=S),
                                       other[:, :].unsqueeze(2).to_broadcast([P, n, S]),
                                       own[:, bass.ds(q, 1), :].to_broadcast([P, n, S]),
                                       ALU.add).then_inc(quad_masks, 1)

            def keep_interest(count):
                pool.wait_ge(z_eps, 1)
                at_least(pool, v_done, count)
                pool.tensor_copy(interest_k[:, :, :], interestT[:, :, :]).then_inc(interest_kept, 1)

            def inverse_deviation(count):
                at_least(pool, z_moments, 2 * count)
                pool.tensor_tensor(rstd[:, 1:2], rstd[:, 0:1], minus_half[:, :], ALU.pow).then_inc(z_rstd, 1)

            def finish_block(count):
                def long_met():
                    pool.wait_ge(z_eps, 1)

                long_met()
                at_least(pool, z_rstd, count)
                pool.tensor_scalar(zn[:, :], z[:, :], moments[:, 0:1], rstd[:, 1:2],
                                   ALU.subtract, ALU.mult).then_inc(z_norm, 1)
                at_least(pool, z_norm, count)
                pool.tensor_tensor(zn[:, :], zn[:, :], lnw_b[:, :], ALU.mult).then_inc(z_scaled, 1)
                at_least(pool, z_scaled, count)
                pool.tensor_tensor(zn[:, :], zn[:, :], lnb_b[:, :], ALU.add).then_inc(z_shifted, 1)
                long_met()
                at_least(pool, z_shifted, count)
                pool.tensor_scalar(y[:, :], zn[:, :], 0.0, ao_c[:, :], ALU.min, ALU.mult).then_inc(z_below, 1)
                long_met()
                at_least(pool, z_below, count)
                pool.tensor_scalar(zn[:, :], zn[:, :], 0.0, None, ALU.max).then_inc(z_above, 1)
                at_least(pool, z_above, count)
                pool.tensor_tensor(y[:, :], y[:, :], zn[:, :], ALU.add).then_inc(y_ready, 1)

            pool.wait_ge(kq_kept, H * C)
            pool.wait_ge(own_ready, 7)
            for k in range(RING):
                quad(k, k)
            pool.wait_ge(ld_rows, 16)
            pool.wait_ge(z_eps, 1)
            with pool.Fori(1, NQ // RING) as it:
                for k in range(RING - 1):
                    quad(it * RING + k, k)
                keep_interest(it)
                quad(it * RING + RING - 1, RING - 1)
                inverse_deviation(it)
                finish_block(it)
                at_least(pool, y_ready, it)
                pool.dma_start(out[bass.ds((it - 1) * P, P), :], y[:, :]).then_inc(stored, 16)
                pool.wait_ge(stored, 16 * it)
            inverse_deviation(BB)

        @block.tensor
        def _(pe):
            def mm(o, l, r, first=True, last=True):
                return pe.matmul(o, l, r, start=first, stop=last, skip_group_check=True)

            def stay_warm(count, into):
                for _i in range(count):
                    pe.transpose(into[:, 0:P], ident[:, :], ident[:, :])

            def prepare_query():
                pe.wait_ge(consts, 1)
                stay_warm(WARM_UP, bank[7])
                pe.wait_ge(ld_query, 16)
                for c in range(C):
                    for j in range(BB):
                        ins = pe.transpose(bank[4 + 2 * c][:, j * P:(j + 1) * P],
                                           query_n[:, j, c * P:(c + 1) * P], ident[:, :])
                    ins.then_inc(query_turned, 1)
                pe.wait_ge(ld_wq, 16)
                for c in range(C):
                    pe.wait_ge(query_kept, 1 + c)
                    for t in range(C):
                        ins = mm(bank[5 + 2 * t][:, :], wqT[:, c, t * P:(t + 1) * P], qT[:, c, :],
                                 c == 0, c == C - 1)
                        if c == C - 1:
                            ins.then_inc(q_done, 1)

            def query_part():
                pe.wait_ge(w1T_ready, 3)
                for c in range(C):
                    for ab in range(2):
                        ins = mm(bank[6][ab * A:(ab + 1) * A, 0:B // 2], w1uT[:, c, :],
                                 view(qT, c * B + ab * GB // 2, [(GB, B // GB), (1, GB // 2)]), c == 0, c == C - 1)
                ins.then_inc(u_done, 1)

            def bias_part():
                pe.wait_ge(bk_ready, 1)
                pe.wait_ge(q_ready, C)
                for t in range(C):
                    for j in range(BB):
                        ins = mm(bank[5][32 * j:32 * j + 32, 0:P], bk_x[:, t, :], q_e[:, t, j * P:(j + 1) * P],
                                 t == 0, t == C - 1)
                ins.then_inc(qbk_done, 1)

            def prepare_heads():
                pe.wait_ge(consts, 15)
                pe.wait_ge(mask_ready, 1)
                pe.wait_ge(hT_ready, 4)
                half = NQ // 2
                log_l, din_l = (to_log[:, :, :, :].rearrange("b g e h -> b (g e h)"),
                                to_din[:, :, :].rearrange("b x e -> b (x e)"))
                mm(bank[0][:, half * S:half * S + GB], log_l, of_group[:, :])
                mm(bank[2][:, half * S:half * S + GB // 2], din_l, of_side[:, :])
                for i in range(4):
                    mm(bank[i][:, 0:half * S], (log_l, din_l)[i // 2],
                       mask_b[:, (i % 2) * half:(i % 2 + 1) * half, :].rearrange("b q s -> b (q s)")
                       ).then_inc(own_done, 1)
                pe.wait_ge(ld_wk, 16)
                pe.wait_ge(u_ready, 1)
                for h in range(H):
                    for c in range(C):
                        i = h * C + c
                        if i >= 2:
                            pe.wait_ge(kq_kept, i - 1)
                        mm(bank[7 - i % 2][:, :], wk_n[:, h // 2, c * P:(c + 1) * P],
                           q_x[:, h % 2, h // 2, :]).then_inc(kq_done, 1)
                pe.wait_ge(ld_late, 16 * 3)
                pe.wait_ge(h1_sum, 1)
                for et in range(C):
                    for c in range(C):
                        ins = mm(bank[4][:, et * D:(et + 1) * D], outw_n[:, c, et * P:(et + 1) * P],
                                 woT[:, C + c, :], c == 0, c == C - 1)
                ins.then_inc(mix_done, 1)
                pe.wait_ge(outb_ready, 1)
                pe.wait_ge(qbk_rows, 1)
                for c in range(C):
                    ins = mm(bank[5][:, 0:D], outb_x[:, c, :], woT[:, C + c, :], c == 0, c == C - 1)
                ins.then_inc(b_mix_done, 1)

            def turn(q, k, r, it, groups=(0, 1)):
                if isinstance(q, int) and q == 1 and r == 0:
                    pe.wait_ge(own_ready, 6)
                pe.wait_ge(ld_hist[k][r], 16 * (it + 1))
                for ab in groups:
                    at_least(pe, hT_ready, 4 * q + 2 * r + ab - 1)
                    for c in range(C):
                        for t in range(NK):
                            ins = pe.transpose(bank[2 * ab + c][:, t * TR:(t + 1) * TR],
                                               hist[0:TR, k, (2 * r + ab) * NK + t, c * P:(c + 1) * P],
                                               ident[0:TR, 0:TR])
                    ins.then_inc(turned, 1)

            def first_layer(q, k, r):
                at_least(pe, qhT_ready, 4 * q + 2 * r + 2)
                if r == 0:
                    at_least(pe, din_masked, q)
                else:
                    at_least(pe, h2_sum, 2 * q)
                for i in range(2 * C):
                    x = (hT[:, k % 2, r], qhT[:, r])[i // C]
                    sides = x[:, i % C, :].rearrange("p (h a n) -> p a h n", h=2, a=2)
                    for ab in range(2):
                        ins = mm(bank[4 + r][ab * A:(ab + 1) * A, 0:GR].rearrange("p (h n) -> p h n", h=2),
                                 w1T[:, i, :], sides[:, ab], i == 0, i == 2 * C - 1)
                ins.then_inc(layer1, 1)

            def second_layer(q, k, r):
                at_least(pe, h1_ready, 2 * q + r + 1)
                mm(bank[4 + r][:, 0:GR], w2T[:, :], h1[:, r, :]).then_inc(layer2, 1)

            def quad_logits(q, k):
                at_least(pe, quad_kq, q + 1)
                at_least(pe, log_masked, q)
                for c in range(C):
                    for g in range(4):
                        ins = mm(bank[6][32 * g:32 * g + 32, 0:GR], kq_quad[:, k % 2, c, 32 * g:32 * g + 32],
                                 hT[:, k % 2, g // 2, c, (g % 2) * GR:(g % 2 + 1) * GR], c == 0, c == C - 1)
                ins.then_inc(logits, 1)

            def quad_scores(q, k):
                at_least(pe, h2_ready, 2 * q + 2)
                for r in range(2):
                    for half in range(2):
                        x = 2 * r + half
                        ins = mm(bank[4][32 * x:32 * x + 32, 0:SIDE], w3_x[:, :],
                                 h2[:, r, half * SIDE:(half + 1) * SIDE])
                ins.then_inc(scores, 1)

            def turn_logits(q, k, it):
                if k == 0:
                    at_least(pe, v_ready, it)
                if k == 1:
                    at_least(pe, z_ready, it)
                at_least(pe, log_probs, q + 1)
                if softmax_bank(q) == 7:
                    at_least(pe, pooledT_ready, q)
                else:
                    pe.wait_ge(hT_ready, 4 * NQ)
                into = bank[softmax_bank(q)]
                for t in range(NK):
                    ins = pe.transpose(into[0:TR, t * P:(t + 1) * P], log_p[:, t * TR:(t + 1) * TR], ident[:, :])
                ins.then_inc(log_pT, 1)

            def turn_scores(q):
                at_least(pe, din_probs, q + 1)
                at_least(pe, log_w, q + 1)
                for t in range(SIDE // TR):
                    ins = pe.transpose(bank[softmax_bank(q)][0:TR, t * P:(t + 1) * P], din_p[:, t * TR:(t + 1) * TR], ident[:, :])
                ins.then_inc(din_pT, 1)

            def pool_rows(q, k):
                at_least(pe, din_w, q + 1)
                for r in range(2):
                    for odd in range(2):
                        for c in range(NK):
                            t = r * (QT // 2) + 2 * c + odd
                            ins = mm(bank[softmax_bank(q)][32 * c:32 * c + 32, r * D:(r + 1) * D],
                                     p_w[0:TR, t, (16, 0)[odd]:(16, 0)[odd] + 32],
                                     hist[0:TR, k, t, :], odd == 0, odd == 1)
                ins.then_inc(pool_done, 1)

            def turn_pooled(q):
                at_least(pe, pooled_ready, q + 1)
                for c in range(C):
                    for r in range(2):
                        ins = pe.transpose(bank[softmax_bank(q)][:, (2 * c + r) * P:(2 * c + r + 1) * P],
                                           pooled[:, r, c * P:(c + 1) * P], ident[:, :])
                ins.then_inc(pooledT, 1)

            def block_values(into, n0=0, n1=P):
                for et in range(C):
                    for c in range(C):
                        for h in (2 * et, 2 * et + 1):
                            ins = mm(into[(h % 2) * HD:(h % 2 + 1) * HD, et * P + n0:et * P + n1],
                                     wvT[:, c, h * HD:(h + 1) * HD],
                                     view(headT, c * P * H + n0 * H + h, [(H, n1 - n0)]), c == 0, c == C - 1)
                ins.then_inc(v_done, 1)

            def mix_interest(into, interest, first):
                for c in range(C):
                    mm(into[:, 0:D], interest[:, c, :], woT[:, c, :], first and c == 0, False)

            def mix_values(into):
                for c in range(C):
                    ins = mm(into[:, 0:D], vT[:, c, :], w_mix[:, c, :], False, c == C - 1)
                ins.then_inc(z_done, 1)

            def step(q, k, it=0):
                one, two = (k - 1) % RING, (k - 2) % RING
                here = lambda back: not isinstance(q, int) or 0 <= q - back < NQ
                if here(0):
                    turn(q, k, 0, it)
                if isinstance(q, int) and q == 0:
                    query_part()
                if isinstance(q, int) and q == 1:
                    pe.wait_ge(w2T_ready, 1)
                    pe.wait_ge(kq_kept, H * C)
                    pe.wait_ge(mix_kept, 1)
                    pe.wait_ge(b_mix_ready, 1)
                if here(1):
                    first_layer(q - 1, one, 1)
                if here(2):
                    turn_scores(q - 2)
                if here(1):
                    second_layer(q - 1, one, 0)
                    quad_logits(q - 1, one)
                    second_layer(q - 1, one, 1)
                if here(2):
                    pool_rows(q - 2, two)
                before_scores = (0, 1) if isinstance(q, int) and q == 1 else (0,)
                if here(0):
                    turn(q, k, 1, it, before_scores)
                if isinstance(q, int) and q == 0:
                    bias_part()
                if here(1):
                    quad_scores(q - 1, one)
                if isinstance(q, int) and q == NQ + 1:
                    stay_warm(STAY_WARM, bank[5])
                if here(2):
                    turn_pooled(q - 2)
                if here(0) and before_scores == (0,):
                    turn(q, k, 1, it, (1,))
                if not isinstance(it, int) and k == 1:
                    at_least(pe, pooledT_ready, RING * it)
                    block_values(bank[7])
                if not isinstance(it, int) and k == 2:
                    at_least(pe, pooledT_ready, q - 1)
                    at_least(pe, interest_kept, it)
                    mix_interest(bank[7], interest_k, True)
                    at_least(pe, v_ready, it)
                    mix_values(bank[7])
                if here(0):
                    first_layer(q, k, 0)
                if here(1):
                    turn_logits(q - 1, one, it)

            prepare_query()
            step(0, 0)
            prepare_heads()
            for k in range(1, RING):
                step(k, k)
            with pe.Fori(1, NQ // RING) as it:
                for k in range(RING):
                    step(it * RING + k, k, it)
            step(NQ, 0)
            pe.wait_ge(pooledT_ready, NQ - 1)
            block_values(bank[2], 0, P - QB)
            mm(bank[0][:, 0:D], ident[:, :], b_mix[:, :], True, False)
            step(NQ + 1, 1)
            stay_warm(STAY_WARM, bank[5])
            pe.wait_ge(pooledT_ready, NQ)
            pe.wait_ge(v_ready, BB)
            block_values(bank[2], P - QB, P)
            mix_interest(bank[0], interestT, False)
            pe.wait_ge(v_ready, BB + 1)
            mix_values(bank[0])

        @block.scalar
        def _(act):
            act.dma_start(columns_c[:, :], columns).then_inc(ld_columns, 16)
            act.dma_start(w1_n[:, :, :, :].rearrange("p f c a -> p (f c) a"),
                          w1_t.rearrange("(i p) a -> p i a", p=P)).then_inc(ld_w1, 16)

            def keep_query():
                for c in range(C):
                    act.wait_ge(query_turned, 1 + c)
                    act.copy(qT[:, c, :], bank[4 + 2 * c][:, :]).then_inc(query_kept, 1)
                act.wait_ge(ld_columns, 16)
                for t in range(C):
                    act.wait_ge(q_done, 1 + t)
                    act.activation(q_e[:, t, :], bank[5 + 2 * t][:, :], ACT.Identity,
                                   bias=inb_c[:, t:t + 1]).then_inc(q_kept, 1)

            def keep_heads():
                for i in range(H * C):
                    act.wait_ge(kq_done, 1 + i)
                    h, c = i // C, i % C
                    act.copy(view(kq, c * B * H + h, [(H, B)]), bank[7 - i % 2][:, :]).then_inc(kq_kept, 1)
                act.wait_ge(mix_done, 1)
                act.copy(w_mix[:, :, :].rearrange("p c e -> p (c e)"), bank[4][:, :]).then_inc(mix_kept, 1)

            def take_turned(q, k, r):
                for ab in range(2):
                    at_least(act, turned, 4 * q + 2 * r + ab + 1)
                    act.copy(view(hT, (((k % 2) * 2 + r) * C) * 2 * GR + ab * GR, [(2 * GR, C), (1, GR)]),
                             psum[:, 2 * ab:2 * ab + 2, 0:GR]).then_inc(hT_ready, 1)

            def add_b2(q, r):
                at_least(act, layer2, 2 * q + r + 1)
                act.activation(h2[:, r, :], bank[4 + r][:, 0:GR], ACT.Identity, bias=b2_s[:, :]).then_inc(h2_sum, 1)

            def exp_logits(q):
                at_least(act, log_masked, q + 1)
                act.activation(log_p[:, :], log_t[:, :], ACT.Exp, bias=small[:, 0:1], scale=-1.0,
                               accum_out=small[:, 1:2]).then_inc(log_exp, 1)

            def exp_scores(q):
                at_least(act, din_masked, q + 1)
                act.activation(din_p[:, :], din_t[:, :], ACT.Exp, bias=small[:, 2:3], scale=-1.0,
                               accum_out=small[:, 3:4]).then_inc(din_exp, 1)

            def take_pooled(q):
                at_least(act, pool_done, q + 1)
                act.copy(pooled[:, :, :].rearrange("p r d -> p (r d)"), bank[softmax_bank(q)][:, :]).then_inc(pooled_ready, 1)

            def take_values(count, src=bank[7], n0=0, n1=P):
                at_least(act, v_done, count)
                for et in range(C):
                    ins = act.activation(vT[:, et, n0:n1], src[:, et * P + n0:et * P + n1], ACT.Identity,
                                         bias=inb_c[:, 2 * C + et:2 * C + et + 1])
                ins.then_inc(v_ready, 1)

            def step(q, k, it=0):
                here = lambda back: not isinstance(q, int) or 0 <= q - back < NQ
                if here(0):
                    take_turned(q, k, 0)
                if here(1):
                    add_b2(q - 1, 0)
                    add_b2(q - 1, 1)
                    exp_logits(q - 1)
                if here(2):
                    take_pooled(q - 2)
                if here(0):
                    take_turned(q, k, 1)
                if here(1):
                    exp_scores(q - 1)
                if not isinstance(it, int) and k == 1:
                    take_values(it)

            keep_query()
            step(0, 0)
            keep_heads()
            for k in range(1, RING):
                step(k, k)
            with act.Fori(1, NQ // RING) as it:
                for k in range(RING):
                    step(it * RING + k, k, it)
            step(NQ, 0)
            take_values(BB, bank[2], 0, P - QB)
            step(NQ + 1, 1)
            take_values(BB + 1, bank[2], P - QB, P)

        @block.vector
        def _(dve):
            for zeros in (w2T[:, :], q_x[:, :, :, :], bk_x[:, :, :], w3_x[:, :], p_w[:, :, :]):
                dve.memset(zeros, 0.0).then_inc(cleared_v, 1)
            dve.wait_ge(ld_columns, 16)
            for i, a in enumerate((a1_c, a2_c)):
                dve.tensor_scalar(sign[:, i:i + 1], a[:, :], 1.0, 2.0, ALU.is_le, ALU.mult).then_inc(signs, 1)
            dve.wait_ge(signs, 2)
            dve.tensor_scalar(sign[:, 3:5], sign[:, 0:2], -1.0, None, ALU.add).then_inc(signs, 1)
            dve.wait_ge(signs, 3)
            sign1, sign2 = sign[:, 3:4], sign[:, 4:5]
            dve.tensor_tensor(sign[:, 5:6], sign1, sign2, ALU.mult).then_inc(signs, 1)
            dve.tensor_tensor(b1_s[:, :], b1_c[:, :], sign1, ALU.mult).then_inc(signs, 1)
            dve.tensor_tensor(b2_s[:, :], b2_c[:, :], sign2, ALU.mult).then_inc(signs, 1)
            dve.wait_ge(signs, 6)
            dve.wait_ge(ld_w1, 16)
            dve.tensor_tensor(w1_c[:, 0, :, :], w1_n[:, 1, :, :], w1_n[:, 2, :, :], ALU.subtract
                              ).then_inc(prepared, 1)
            dve.tensor_tensor(w1_c[:, 1, :, :], w1_n[:, 0, :, :], w1_n[:, 2, :, :], ALU.add).then_inc(prepared, 1)
            dve.wait_ge(prepared, 2)
            for dst, src in ((w1T[:, 0:C, :], w1_c[:, 0, :, :]), (w1T[:, C:2 * C, :], w1_n[:, 3, :, :]),
                             (w1uT[:, :, :], w1_c[:, 1, :, :])):
                dve.tensor_scalar(dst, src, sign1, None, ALU.mult).then_inc(w1T_ready, 1)
            dve.wait_ge(cleared_v, 5)
            for r in range(2):
                side = slice(r * A, (r + 1) * A)
                ins = dve.tensor_scalar(w2T[side, side], w2_c[side, :], sign[side, 5:6], None, ALU.mult)
            ins.then_inc(w2T_ready, 1)
            for r in range(2):
                side = slice(r * A, (r + 1) * A)
                dve.tensor_scalar(w3_x[side, 16 * r:16 * r + GB // 2], w3_c[side, :].to_broadcast([A, GB // 2]),
                                  sign[side, 4:5], None, ALU.mult)
            for h in range(H):
                side = slice(h % 2 * HD, (h % 2 + 1) * HD)
                ins = dve.tensor_copy(bk_x[side, h // 2, h:h + 1], inb_c[side, C + h // 2:C + h // 2 + 1])
            ins.then_inc(bk_ready, 1)
            dve.wait_ge(ld_mask, 16)
            dve.tensor_scalar(mask_b[:, :, :], mask_i[:, :, :], 0.0, -1.0, ALU.not_equal,
                              ALU.add).then_inc(mask_ready, 1)
            for t in range(C):
                dve.wait_ge(q_kept, 1 + t)
                for r in range(2):
                    side = slice(r * HD, (r + 1) * HD)
                    ins = dve.tensor_scalar(q_x[side, r, t, :], bank[5 + 2 * t][side, :], inb_c[side, t:t + 1],
                                            None, ALU.add)
                ins.then_inc(q_ready, 1)

            def keep_query_part():
                dve.wait_ge(u_done, 1)
                dve.tensor_scalar(u[:, :, :].rearrange("p n e -> p (n e)"), bank[6][:, 0:B // 2], b1_s[:, :], None,
                                  ALU.add).then_inc(u_ready, 1)
                dve.wait_ge(qbk_done, 1)
                dve.tensor_copy(qbk_r[:, :, :], bank[5][:, 0:P].rearrange("p (q b) -> p b q", b=QB)
                                ).then_inc(qbk_rows, 1)
                dve.wait_ge(u_ready, 1)

            def keep_heads():
                dve.tensor_copy(outb_x[:, :, :], outb_c[:, :].unsqueeze(2).to_broadcast([P, C, P])
                                ).then_inc(outb_ready, 1)
                half = NQ // 2
                dve.wait_ge(own_done, 4)
                for i in range(2):
                    dve.tensor_scalar(own_din[:, i * half:(i + 1) * half, :],
                                      bank[2 + i][:, 0:half * S].rearrange("p (q s) -> p q s", s=S), BIG,
                                      b3_c[:, :], ALU.mult, ALU.add).then_inc(own_ready, 1)
                for m, src in ((other_log[:, :], bank[0][:, half * S:half * S + GB]),
                               (other_din[:, :], bank[2][:, half * S:half * S + GB // 2])):
                    dve.tensor_scalar(m, src, -1.0, BIG, ALU.add, ALU.mult).then_inc(own_ready, 1)
                for i in range(2):
                    dve.tensor_scalar(own_log[:, i * half:(i + 1) * half, :],
                                      bank[i][:, 0:half * S].rearrange("p (q s) -> p q s", s=S), BIG,
                                      None, ALU.mult).then_inc(own_ready, 1)
                dve.wait_ge(own_ready, 6)
                dve.wait_ge(qbk_moved, 16 * H * BB)
                dve.tensor_tensor(own_log[:, :, :], own_log[:, :, :],
                                  qbk[:, :].unsqueeze(2).to_broadcast([P, NQ, S]), ALU.add).then_inc(own_ready, 1)
                dve.wait_ge(ld_rows, 16)
                dve.wait_ge(b_mix_done, 1)
                dve.tensor_tensor(b_mix[:, :], bank[5][:, 0:D], bo_b[:, :], ALU.add).then_inc(b_mix_ready, 1)

            def times_query(q, k, r):
                for ab in range(2):
                    g = 4 * q + 2 * r + ab
                    at_least(dve, hT_ready, g + 1)
                    off, dims = r * C * 2 * GR + ab * GR, [(2 * GR, C), (S, GB), (1, S)]
                    dve.tensor_tensor(view(qhT, off, dims), view(hT, (k % 2) * 2 * C * 2 * GR + off, dims),
                                      qT[:, :, bass.ds(g * GB, GB)].unsqueeze(3).to_broadcast([P, C, GB, S]),
                                      ALU.mult).then_inc(qhT_ready, 1)

            def add_query(q, r):
                at_least(dve, layer1, 2 * q + r + 1)
                dve.tensor_tensor(h1[:, r, :].rearrange("p (e s) -> p e s", s=S),
                                  bank[4 + r][:, 0:GR].rearrange("p (e s) -> p e s", s=S),
                                  u[:, bass.ds(2 * q + r, 1), :].rearrange("p n e -> p (n e)").unsqueeze(2)
                                  .to_broadcast([P, GB, S]), ALU.add).then_inc(h1_sum, 1)

            def prelu1(q, r):
                at_least(dve, h1_sum, 2 * q + r + 1)
                dve.scalar_tensor_tensor(h1[:, r, :], h1[:, r, :], a1_c[:, :], h1[:, r, :], ALU.mult,
                                         ALU.max).then_inc(h1_ready, 1)

            def prelu2(q, r):
                at_least(dve, h2_sum, 2 * q + r + 1)
                dve.scalar_tensor_tensor(h2[:, r, :], h2[:, r, :], a2_c[:, :], h2[:, r, :], ALU.mult,
                                         ALU.max).then_inc(h2_ready, 1)

            def mask_logits(q, k):
                dve.wait_ge(qbk_moved, 16 * H * BB)
                at_least(dve, logits, q + 1)
                at_least(dve, quad_masks, 2 * q + 2)
                dve.tensor_tensor_reduce(log_t[:, :], bank[6][:, 0:GR], mask_log[:, k % 2, :],
                                         -1.0 / HD ** 0.5, 3e38, ALU.add, ALU.min,
                                         small[:, 0:1]).then_inc(log_masked, 1)

            def mask_scores(q, k):
                dve.wait_ge(qbk_moved, 16 * H * BB)
                at_least(dve, scores, q + 1)
                at_least(dve, quad_masks, 2 * q + 2)
                dve.tensor_tensor_reduce(din_t[:, :], bank[4][:, 0:SIDE], mask_din[:, k % 2, :], -1.0, 3e38,
                                         ALU.add, ALU.min, small[:, 2:3]).then_inc(din_masked, 1)

            def normalise_logits(q):
                at_least(dve, log_exp, q + 1)
                dve.reciprocal(small[:, 4:5], small[:, 1:2]).then_inc(recips, 1)
                at_least(dve, recips, 2 * q + 1)
                dve.tensor_scalar(log_p[:, :], log_p[:, :], small[:, 4:5], None, ALU.mult).then_inc(log_probs, 1)

            def normalise_scores(q):
                at_least(dve, din_exp, q + 1)
                dve.reciprocal(small[:, 5:6], small[:, 3:4]).then_inc(recips, 1)
                at_least(dve, recips, 2 * q + 2)
                dve.tensor_scalar(din_p[:, :], din_p[:, :], small[:, 5:6], None, ALU.mult).then_inc(din_probs, 1)

            def place_logits(q):
                at_least(dve, log_pT, q + 1)
                dve.tensor_copy(view(p_w, 16, [(NK * PW, 4), (PW, NK), (1, 8)], TR),
                                view(psum, softmax_bank(q) * 512, [(32, 4), (P + 8, NK), (1, 8)], TR)).then_inc(log_w, 1)

            def place_scores(q):
                at_least(dve, din_pT, q + 1)
                dve.tensor_copy(view(p_w, 24, [(2 * PW, QT // 2), (PW, 2), (1, 2)], TR),
                                view(psum, softmax_bank(q) * 512, [(16, QT // 2), (P + 2, 2), (1, 2)], TR)).then_inc(din_w, 1)

            def take_pooledT(q, k, it):
                if k == 0:
                    at_least(dve, v_done, it)
                    at_least(dve, interest_kept, it)
                at_least(dve, pooledT, q + 1)
                src = bank[softmax_bank(q)][:, :].rearrange("p (c t x) -> p c t x", c=C, x=16)
                dve.tensor_copy(headT[:, :, k * P:(k + 1) * P].rearrange("p c (t x) -> p c t x", x=8),
                                src[:, :, :, 0:8])
                dve.tensor_copy(interestT[:, :, k * QB:(k + 1) * QB].rearrange("p c (t x) -> p c t x", x=2),
                                src[:, :, :, 8:10]).then_inc(pooledT_ready, 1)

            def block_moments(count):
                at_least(dve, z_done, count)
                dve.tensor_tensor(z[:, :], bank[7][:, 0:D], b_mix[:, :], ALU.add).then_inc(z_ready, 1)
                at_least(dve, z_ready, count)
                dve.bn_stats(stats[:, :], z[:, :]).then_inc(z_stats, 1)
                dve.wait_ge(qbk_moved, 16 * H * BB)
                at_least(dve, z_stats, count)
                dve.bn_aggr(moments[:, :], stats[:, :]).then_inc(z_moments, 1)
                at_least(dve, z_moments, 2 * count - 1)
                dve.tensor_scalar(rstd[:, 0:1], moments[:, 1:2], EPS, None, ALU.add).then_inc(z_moments, 1)

            def step(q, k, it=0):
                one = (k - 1) % RING
                here = lambda back: not isinstance(q, int) or 0 <= q - back < NQ
                if isinstance(q, int) and q == 0:
                    dve.wait_ge(query_kept, C)
                if here(0):
                    times_query(q, k, 0)
                if isinstance(q, int) and q == 0:
                    keep_query_part()
                if here(1):
                    add_query(q - 1, 1)
                if here(2):
                    place_scores(q - 2)
                if here(1):
                    prelu1(q - 1, 1)
                    prelu2(q - 1, 0)
                    mask_logits(q - 1, one)
                    prelu2(q - 1, 1)
                    normalise_logits(q - 1)
                    mask_scores(q - 1, one)
                if here(2):
                    take_pooledT(q - 2, (k - 2) % RING, it)
                if here(0):
                    times_query(q, k, 1)
                if here(1):
                    normalise_scores(q - 1)
                if not isinstance(it, int) and k == 2:
                    block_moments(it)
                if here(0):
                    add_query(q, 0)
                if here(1):
                    place_logits(q - 1)
                if here(0):
                    prelu1(q, 0)

            step(0, 0)
            keep_heads()
            for k in range(1, RING):
                step(k, k)
            with dve.Fori(1, NQ // RING) as it:
                for k in range(RING):
                    step(it * RING + k, k, it)
            step(NQ, 0, 0)
            step(NQ + 1, 1, 0)
            z_last = bank[0][:, 0:D]
            dve.wait_ge(z_done, BB)
            dve.bn_stats(stats[:, :], z_last).then_inc(z_stats, 1)
            dve.wait_ge(y_ready, BB - 1)
            dve.wait_ge(stored, 16 * (BB - 1))
            dve.wait_ge(z_stats, BB)
            dve.bn_aggr(moments[:, :], stats[:, :]).then_inc(z_moments, 1)
            dve.wait_ge(z_moments, 2 * BB - 1)
            dve.tensor_scalar(rstd[:, 0:1], moments[:, 1:2], EPS, None, ALU.add).then_inc(z_moments, 1)
            dve.scalar_tensor_tensor(zn[:, :], z_last, moments[:, 0:1], lnw_b[:, :], ALU.subtract,
                                     ALU.mult).then_inc(z_norm, 1)
            dve.wait_ge(z_norm, BB)
            dve.wait_ge(z_rstd, BB)
            dve.scalar_tensor_tensor(zn[:, :], zn[:, :], rstd[:, 1:2], lnb_b[:, :], ALU.mult,
                                     ALU.add).then_inc(z_shifted, 1)
            dve.wait_ge(z_shifted, BB)
            dve.tensor_scalar(y[:, :], zn[:, :], 0.0, ao_c[:, :], ALU.min, ALU.mult).then_inc(z_below, 1)
            dve.wait_ge(z_below, BB)
            dve.scalar_tensor_tensor(y[:, :], zn[:, :], 0.0, y[:, :], ALU.max, ALU.add).then_inc(y_ready, 1)


def kernel(**inputs):
    import numpy as _np
    import concourse.bacc as _bacc
    from concourse import mybir as _mybir
    from concourse.bass_utils import run_bass_kernel_spmd as _run

    x = {name: _np.asarray(a) for name, a in inputs.items()}
    par = {name[len("L0_rec_"):]: a for name, a in x.items() if name.startswith("L0_rec_")}
    D = par["query"].shape[1]
    P = 128

    def on_partitions(a):
        a = a.reshape(-1)
        return a.reshape(-1, P).T if a.size > P else _np.tile(a, P // a.size)[:, None]

    in_w = par["in_w"]
    columns = _np.concatenate([_np.concatenate([par["W2"].T, par["W2"].T])] + [
        on_partitions(par[name]) for name in ("b1", "b2", "W3", "a1", "a2", "ao", "b3", "in_b", "out_b")], axis=1)
    laid_out = dict(
        mask=x["r_history_mask"], query=par["query"], history=par["history"], w1_t=par["W1"].T,
        wq_t=in_w[0:D].T, wk=in_w[D:2 * D], wv_t=in_w[2 * D:3 * D].T, out_w=par["out_w"], wo_t=par["Wo"].T,
        columns=columns, rows=_np.stack([par["bo"], par["ln_w"], par["ln_b"]]))

    nc = _bacc.Bacc("TRN2", target_bir_lowering=False, num_devices=1)
    arrays, args = {}, []
    for name, a in laid_out.items():
        a = _np.ascontiguousarray(a)
        arrays[f"in_{name}_dram"] = a
        args.append(nc.dram_tensor(f"in_{name}_dram", a.shape, _mybir.dt.from_np(a.dtype), kind="ExternalInput").ap())
    args.append(nc.dram_tensor("out_0_dram", par["query"].shape, F32, kind="ExternalOutput").ap())
    rec_kernel(nc, *args)
    r = _run(nc, [arrays], core_ids=[0])
    return r.results[0]["out_0_dram"]
```
